# Optimizing a Trainium2 kernel written in Bass

```python
import numpy as np
import jax
import jax.numpy as jnp

def _softmax(x, axis=-1):
    return jax.nn.softmax(x, axis=axis)

def _gelu(x):
    return jax.nn.gelu(x, approximate=True)

def _silu(x):
    return jax.nn.silu(x)

def _sigmoid(x):
    return jax.nn.sigmoid(x)

def _layernorm(x, axis=-1, eps=1e-05):
    m = jnp.mean(x, axis=axis, keepdims=True)
    v = jnp.var(x, axis=axis, keepdims=True)
    return (x - m) / jnp.sqrt(v + eps)

def _scatter_add(tgt, idx, src, axis=0):
    return tgt.at[idx].add(src)

def _segment_sum(src, seg, n):
    return jax.ops.segment_sum(src, seg, n)
kernel_name = 'mk_decoder_preln_d1_seqx_r4_27b6a4'

def setup_inputs(seed: int=0):
    np.random.seed(seed)
    _w = jnp.asarray

    def _rec_inputs():
        import jax
        import jax.numpy as jnp
        _rk = jax.random.key(seed)
        x = -0.0002928 + 1 * jax.random.normal(jax.random.fold_in(_rk, 1), (64, 128, 256), jnp.float32)
        _lenS = 128 - jax.random.randint(jax.random.fold_in(_rk, 7), (64,), 0, max(1, 128 // 4) + 1, jnp.int32)
        _lenS2 = 128 - jax.random.randint(jax.random.fold_in(_rk, 8), (64,), 0, max(1, 128 // 4) + 1, jnp.int32)
        _ctx_1024P = jax.random.normal(jax.random.fold_in(_rk, 11), (64, 16, 256), jnp.float32)
        _ctx_1024c = jax.random.dirichlet(jax.random.fold_in(_rk, 511), 0.3 * jnp.ones((16,), jnp.float32), (64, 128))
        _ctx_1024t = jnp.einsum('bsk,bkd->bsd', _ctx_1024c, _ctx_1024P)
        _ctx_1024t = _ctx_1024t * jax.lax.rsqrt(jnp.mean(jnp.square(_ctx_1024t)) + 1e-12) * 0.953939
        ctx_1024 = -1.39393e-06 + 0.999914 * (_ctx_1024t + 0.3 * jax.random.normal(jax.random.fold_in(_rk, 611), (64, 128, 256), jnp.float32))
        fside_Bx1xSxS2_0 = -4.48278e-06 + 1.00019 * jax.random.normal(jax.random.fold_in(_rk, 12), (64, 1, 128, 128), jnp.float32)
        return (x, ctx_1024, fside_Bx1xSxS2_0)
    x, ctx_1024, fside_Bx1xSxS2_0 = _rec_inputs()

    def _L0_attn_setup():
        import jax, jax.numpy as jnp
        import numpy as np
        B, S, D = (4, 512, 256)
        COMP_RATIO = 4
        TOP_K = 64
        key = jax.random.key(seed)
        ks = jax.random.split(key, 9)
        sd = 1.0 / np.sqrt(D)
        return {'x': jax.random.normal(ks[0], (B, S, D), dtype=jnp.float32), 'Wq': jax.random.normal(ks[1], (D, D), dtype=jnp.float32) * sd, 'bq': jnp.zeros((D,), dtype=jnp.float32), 'Wk': jax.random.normal(ks[2], (D, D), dtype=jnp.float32) * sd, 'bk': jnp.zeros((D,), dtype=jnp.float32), 'Wv': jax.random.normal(ks[3], (D, D), dtype=jnp.float32) * sd, 'bv': jnp.zeros((D,), dtype=jnp.float32), 'Wo': jax.random.normal(ks[4], (D, D), dtype=jnp.float32) * sd, 'bo': jnp.zeros((D,), dtype=jnp.float32)}
    _L0_attn_all = _L0_attn_setup()
    _L0_attn_in = {k: v for k, v in _L0_attn_all.items() if k in ('Wq', 'bq', 'Wk', 'bk', 'Wv', 'bv', 'Wo', 'bo')}
    del _L0_attn_all

    def _L0_xattn_setup():
        import jax, jax.numpy as jnp
        import numpy as np
        B, S, D_FF = (2, 512, 256)
        NUM_HEADS, D_KV = (16, 64)
        INNER = NUM_HEADS * D_KV
        key = jax.random.key(seed)
        ks = jax.random.split(key, 8)
        scale = 1.0 / np.sqrt(D_FF)
        return {'q': jax.random.normal(ks[0], (B, S, D_FF), jnp.float32), 'k': jax.random.normal(ks[1], (B, S, D_FF), jnp.float32), 'v': jax.random.normal(ks[2], (B, S, D_FF), jnp.float32), 'attn_mask': jax.random.normal(ks[3], (B, 1, S, S), jnp.float32), 'Wq': jax.random.normal(ks[4], (INNER, D_FF), jnp.float32) * scale, 'Wk': jax.random.normal(ks[5], (INNER, D_FF), jnp.float32) * scale, 'Wv': jax.random.normal(ks[6], (INNER, D_FF), jnp.float32) * scale, 'Wo': jax.random.normal(ks[7], (D_FF, INNER), jnp.float32) * scale, 'num_heads': NUM_HEADS}
    _L0_xattn_all = _L0_xattn_setup()
    _L0_xattn_in = {k: v for k, v in _L0_xattn_all.items() if k in ('Wq', 'Wk', 'Wv', 'Wo')}
    del _L0_xattn_all

    def _L0_ffn_setup():
        import jax, jax.numpy as jnp
        import numpy as np
        QP = 127.0
        MIN_RANGE = 1e-06

        def _ste_round(x):
            return x + jax.lax.stop_gradient(jnp.round(x) - x)

        def _quant_per_tensor(x):
            scale = jnp.maximum(jnp.max(jnp.abs(x)), MIN_RANGE) / QP
            return (_ste_round(x / scale), scale)

        def _qlinear(x2d, w, b):
            xq, sx = _quant_per_tensor(x2d)
            wq, sw = _quant_per_tensor(w)
            out = jnp.matmul(xq, wq.T) + b[None, :]
            return out * (sw * sx)
        key = jax.random.key(seed)
        k = jax.random.split(key, 5)
        B, N, D, H = (8, 256, 256, 1024)
        return {'x': jax.random.normal(k[0], (B, N, D), dtype=jnp.float32), 'w1': jax.random.normal(k[1], (H, D), dtype=jnp.float32) * 0.02, 'b1': jax.random.normal(k[2], (H,), dtype=jnp.float32) * 0.02, 'w2': jax.random.normal(k[3], (D, H), dtype=jnp.float32) * 0.02, 'b2': jax.random.normal(k[4], (D,), dtype=jnp.float32) * 0.02}
    _L0_ffn_all = _L0_ffn_setup()
    _L0_ffn_in = {k: v for k, v in _L0_ffn_all.items() if k in ('w1', 'b1', 'w2', 'b2')}
    del _L0_ffn_all
    return {'x': x, 'ctx_1024': ctx_1024, 'fside_Bx1xSxS2_0': fside_Bx1xSxS2_0, 'L0_attn_Wq': _L0_attn_in['Wq'], 'L0_attn_bq': _L0_attn_in['bq'], 'L0_attn_Wk': _L0_attn_in['Wk'], 'L0_attn_bk': _L0_attn_in['bk'], 'L0_attn_Wv': _L0_attn_in['Wv'], 'L0_attn_bv': _L0_attn_in['bv'], 'L0_attn_Wo': _L0_attn_in['Wo'], 'L0_attn_bo': _L0_attn_in['bo'], 'L0_xattn_Wq': _L0_xattn_in['Wq'], 'L0_xattn_Wk': _L0_xattn_in['Wk'], 'L0_xattn_Wv': _L0_xattn_in['Wv'], 'L0_xattn_Wo': _L0_xattn_in['Wo'], 'L0_ffn_w1': _L0_ffn_in['w1'], 'L0_ffn_b1': _L0_ffn_in['b1'], 'L0_ffn_w2': _L0_ffn_in['w2'], 'L0_ffn_b2': _L0_ffn_in['b2']}

def reference(x, ctx_1024, fside_Bx1xSxS2_0, L0_attn_Wq, L0_attn_bq, L0_attn_Wk, L0_attn_bk, L0_attn_Wv, L0_attn_bv, L0_attn_Wo, L0_attn_bo, L0_xattn_Wq, L0_xattn_Wk, L0_xattn_Wv, L0_xattn_Wo, L0_ffn_w1, L0_ffn_b1, L0_ffn_w2, L0_ffn_b2):
    import jax
    import jax.numpy as jnp

    def _L0_attn_ref(x, Wq, bq, Wk, bk, Wv, bv, Wo, bo):
        import jax, jax.numpy as jnp
        import numpy as np
        B, S, D = (4, 512, 256)
        COMP_RATIO = 4
        TOP_K = 64
        b, s, d = x.shape
        scale = 1.0 / jnp.sqrt(jnp.asarray(d, x.dtype))
        Q = x @ Wq + bq
        K = x @ Wk + bk
        V = x @ Wv + bv
        raw = jnp.einsum('bqd,bkd->bqk', Q, K) * scale
        causal = jnp.triu(jnp.ones((s, s), dtype=bool), k=1)
        w_scores = jnp.where(causal, jnp.asarray(-jnp.inf, raw.dtype), raw)
        w_attn = jax.nn.softmax(w_scores, axis=-1) @ V
        sc = s // COMP_RATIO
        Kc = K.reshape(b, sc, COMP_RATIO, d).mean(axis=2)
        Vc = V.reshape(b, sc, COMP_RATIO, d).mean(axis=2)
        c_scores = jnp.einsum('bqd,bkd->bqk', Q, Kc) * scale
        c_attn = jax.nn.softmax(c_scores, axis=-1) @ Vc
        top_vals, top_idx = jax.lax.top_k(raw, TOP_K)
        bi = jnp.arange(b)[:, None, None]
        si = jnp.arange(s)[None, :, None]
        sparse = jnp.zeros_like(raw).at[bi, si, top_idx].set(top_vals)
        s_attn = jax.nn.softmax(sparse, axis=-1) @ V
        out = (w_attn + c_attn + s_attn) / 3.0
        return out @ Wo + bo

    def _L0_xattn_ref(q, k, v, attn_mask, Wq, Wk, Wv, Wo, num_heads):
        import jax, jax.numpy as jnp
        import numpy as np
        B, S, D_FF = (2, 512, 256)
        NUM_HEADS, D_KV = (16, 64)
        INNER = NUM_HEADS * D_KV
        b, s, _ = q.shape

        def proj_heads(x, W):
            y = jnp.einsum('bsd,ed->bse', x, W)
            return y.reshape(b, s, num_heads, -1).transpose(0, 2, 1, 3)
        qh = proj_heads(q, Wq)
        kh = proj_heads(k, Wk)
        vh = proj_heads(v, Wv)
        scores = jnp.einsum('bhqd,bhkd->bhqk', qh, kh) + attn_mask
        probs = jax.nn.softmax(scores, axis=-1)
        ctx = jnp.einsum('bhqk,bhkd->bhqd', probs, vh)
        ctx = ctx.transpose(0, 2, 1, 3).reshape(b, s, -1)
        return jnp.einsum('bse,de->bsd', ctx, Wo)

    def _L0_ffn_ref(x, w1, b1, w2, b2):
        import jax, jax.numpy as jnp
        import numpy as np
        QP = 127.0
        MIN_RANGE = 1e-06

        def _ste_round(x):
            return x + jax.lax.stop_gradient(jnp.round(x) - x)

        def _quant_per_tensor(x):
            scale = jnp.maximum(jnp.max(jnp.abs(x)), MIN_RANGE) / QP
            return (_ste_round(x / scale), scale)

        def _qlinear(x2d, w, b):
            xq, sx = _quant_per_tensor(x2d)
            wq, sw = _quant_per_tensor(w)
            out = jnp.matmul(xq, wq.T) + b[None, :]
            return out * (sw * sx)
        B, N, D = x.shape
        h = _qlinear(x.reshape(-1, D), w1, b1)
        h = jax.nn.gelu(h, approximate=False)
        o = _qlinear(h, w2, b2)
        return o.reshape(B, N, -1)
    x = x + _L0_attn_ref(_layernorm(x, axis=-1), L0_attn_Wq, L0_attn_bq, L0_attn_Wk, L0_attn_bk, L0_attn_Wv, L0_attn_bv, L0_attn_Wo, L0_attn_bo)
    x = x + _L0_xattn_ref(_layernorm(x, axis=-1), ctx_1024, ctx_1024, fside_Bx1xSxS2_0, L0_xattn_Wq, L0_xattn_Wk, L0_xattn_Wv, L0_xattn_Wo, 16)
    x = x + _L0_ffn_ref(_layernorm(x, axis=-1), L0_ffn_w1, L0_ffn_b1, L0_ffn_w2, L0_ffn_b2)
    return x

_drawn_inputs = setup_inputs


def setup_inputs(seed=0):
    import zlib

    import numpy as np

    out = dict(_drawn_inputs(seed))
    spreads = {'L0_attn_bq': (0.0, 0.395),
     'L0_attn_bk': (0.0, 2.0),
     'L0_attn_bv': (0.0, 0.1),
     'L0_attn_bo': (0.0, 0.1)}
    factors = {'L0_ffn_b1': 64.0, 'L0_ffn_b2': 64.0}
    for name, (base, spread) in spreads.items():
        noise = np.random.default_rng([zlib.crc32(name.encode()), seed]).standard_normal(out[name].shape)
        drawn = base * np.exp(spread * noise) if base else spread * noise
        out[name] = jnp.asarray(drawn.astype(out[name].dtype))
    for name, factor in factors.items():
        out[name] = (out[name] * factor).astype(out[name].dtype)
    return out
```

```python
from contextlib import ExitStack

import concourse.bass as bass
from concourse import mybir

F32 = mybir.dt.float32
F32R = mybir.dt.float32r
F16 = mybir.dt.float16
BF16 = mybir.dt.bfloat16
ALU = mybir.AluOpType
ACT = mybir.ActivationFunctionType
AX = mybir.AxisListType.X
RMAX = bass.bass_isa.ReduceOp.max

P = 128
D = 256
DT = D // P
NB = 64
PAIRS = NB // 2
HEADS = 16
DH = 64
INNER = HEADS * DH
ET = INNER // P
GROUP = 4
TOP_K = 64
QUAD = 4
QUADS = 2 * HEADS // QUAD
VW = DH + 2
FW = D + 2
NEG = -3.0e38
MASKED = -1.0e30
EPS = 1e-5
QP = 127.0
MIN_RANGE = 1e-6
MAGIC = 12582912.0
HI, LO = 0, 1
FREE = 2

(J_X1, J_CTX, J_Q0, J_K0, J_Q1, J_K1, J_Q2, J_Q3, J_K2, J_K3, J_X, J_G, J_VV0, J_VV1, J_PT0, J_PT1,
 J_AO, J_V0, J_V1, J_VV2, J_RAW, J_VV3) = range(22)
FJ = 22
J_Q, J_K = (J_Q0, J_Q1, J_Q2, J_Q3), (J_K0, J_K1, J_K2, J_K3)
J_VV = (J_VV0, J_VV1, J_VV2, J_VV3)
OF_LAST_PAIR = (J_X1, *J_Q)
OF_NEXT_PAIR = (J_X, J_G, J_V0, J_V1, J_RAW)
WITH_HI = [k for k in range(FJ) if k not in (J_RAW, J_AO)]
BACK = ["pv0", "pv1", "pv2", "ct0", "pv3", "ct1", "pv4", "pv5", "out0", "pv6", "ct2", "pv7", "ct3", "out1"]
BJ = len(BACK)


def runs(k, front, back, ahead):
    return back if k in OF_LAST_PAIR else ahead if k in OF_NEXT_PAIR else front


def left_out(k, jobs, *halves):
    before = jobs[:jobs.index(k)]
    return next((n for n, m in enumerate(reversed(before)) if runs(m, *halves)), len(before))


def steps(k, jobs, *halves):
    after = jobs[jobs.index(k) + 1:]
    return 1 + left_out(k, jobs, *halves) + (0 if any(runs(m, *halves) for m in after) else len(after))


def wait_apart(eng, sem, value):
    value = value if isinstance(value, int) else eng.to_reg(value)
    eng.wait_ge(sem, 1)
    eng.wait_ge(sem, value)


def split_products(pe, out, lhs, rhs, last=True, first=True):
    pe.matmul(out, lhs[HI], rhs[HI], start=first, stop=False)
    pe.matmul(out, lhs[HI], rhs[LO], start=False, stop=False)
    return pe.matmul(out, lhs[LO], rhs[HI], start=False, stop=last)


def prepare_weights(nc, dram, keep, psum):
    with ExitStack() as ctx:
        def sb(name, shape, dt=F32):
            return ctx.enter_context(nc.sbuf_tensor(name, shape, dt))

        def sem(name):
            return ctx.enter_context(nc.semaphore(name))

        attn_w = {n: sb(f"w_{n}", [P, DT, D]) for n in ("Wq", "Wk", "Wv", "Wo")}
        attn_t = {n: sb(f"wt_{n}", [P, DT, D]) for n in ("Wq", "Wk", "Wv")}
        cross = {n: sb(f"cw_{n}", [P, ET, D]) for n in ("Wq", "Wk", "Wv")}
        cross_o = sb("cw_Wo", [P, DT, INNER])
        w1 = sb("w1_nat", [P, ET, D])
        w2 = sb("w2_nat", [P, DT, INNER])
        bias = {n: sb(f"b_{n}", [P, DT]) for n in ("bq", "bk", "bv")}
        bias_rows = {n: sb(f"br_{n}", [P, DT, P]) for n in ("bq", "bv")}
        wabs = sb("wabs", [P, 2])
        wmax = sb("wmax", [P, 2])
        winv = sb("winv", [P, 2])

        attn_loaded = sem("attn_loaded")
        bias_loaded = sem("bias_loaded")
        cross_loaded = sem("cross_loaded")
        ffn_loaded = sem("ffn_loaded")
        ident_zero, ident_ready = sem("ident_zero"), sem("ident_ready")
        causal_zero, causal_ready = sem("causal_zero"), sem("causal_ready")
        rows_ready = sem("rows_ready")
        job_full, job_hi, job_done = sem("job_full"), sem("job_hi"), sem("job_done")
        abs_ready, abs_all = sem("abs_ready"), sem("abs_all")
        scale_step = sem("scale_step")
        quant_step, quantised = sem("quant_step"), sem("quantised")
        u_hi = sem("u_hi")
        bank_of = lambda n: psum[:, n % 4, :]

        N_T, N_A, N_VO, N_COL, N_ROW, N_CROSS, N_FFN, N_JOBS = 0, 3, 4, 5, 6, 7, 23, 31
        TWICE = [N_A, N_VO] + list(range(N_CROSS, N_FFN))
        hi_count = lambda n: TWICE.index(n) + 1
        cross_jobs = [(n, kt, g) for n in ("Wq", "Wk", "Wv") for kt in range(DT) for g in range(2)]

        block = ctx.enter_context(nc.Block())

        @block.sync
        def _(sp):
            for n in ("Wq", "Wk", "Wv", "Wo"):
                sp.dma_start(attn_w[n][:], dram["attn_" + n].rearrange("(t p) e -> p t e", p=P)).then_inc(attn_loaded, 16)
            for n in ("Wq", "Wk", "Wv"):
                sp.dma_start(cross[n][:], dram["xattn_" + n].rearrange("(t p) d -> p t d", p=P)).then_inc(cross_loaded, 16)
            sp.dma_start(cross_o[:], dram["xattn_Wo"].rearrange("(t p) e -> p t e", p=P)).then_inc(cross_loaded, 16)
            sp.wait_ge(bias_loaded, 16 * 6)

        @block.gpsimd
        def _(pool):
            pool.memset(keep["ident"][:], 0.0).then_inc(ident_zero, 1)
            pool.memset(keep["causal"][:], 0.0).then_inc(causal_zero, 1)
            pool.wait_ge(ident_zero, 1)
            pool.affine_select(out=keep["ident"][:], in_=keep["ident"][:], compare_op=ALU.not_equal, fill=1.0,
                               base=0, pattern=[[-1, P]], channel_multiplier=1).then_inc(ident_ready, 1)
            pool.wait_ge(causal_zero, 1)
            pool.affine_select(out=keep["causal"][:], in_=keep["causal"][:], compare_op=ALU.is_ge, fill=MASKED,
                               base=0, pattern=[[-1, P]], channel_multiplier=1).then_inc(causal_ready, 1)
            pool.memset(keep["half4"][:], -0.5)
            for k in range(2):
                pool.wait_ge(abs_ready, k + 1)
                pool.partition_all_reduce(wmax[:, k:k + 1], wabs[:, k:k + 1], P, RMAX).then_inc(abs_all, 1)
            pool.wait_ge(causal_ready, 1)

        @block.scalar
        def _(act):
            with nc.allow_non_contiguous_dma(reason="bias columns"):
                for n in ("bq", "bk", "bv"):
                    act.dma_start(bias[n][:], dram["attn_" + n].rearrange("(t p) -> p t", p=P)).then_inc(bias_loaded, 16)
                act.dma_start(keep["bo_row"][:], dram["attn_bo"].rearrange("(a d) -> a d", a=1).to_broadcast([P, D])).then_inc(bias_loaded, 16)
                act.dma_start(keep["b1_col"][:], dram["ffn_b1"].rearrange("(t p) -> p t", p=P)).then_inc(bias_loaded, 16)
                act.dma_start(keep["b2_row"][:], dram["ffn_b2"].rearrange("(a d) -> a d", a=1).to_broadcast([P, D])).then_inc(bias_loaded, 16)
            act.dma_start(w1[:], dram["ffn_w1"].rearrange("(t p) d -> p t d", p=P)).then_inc(ffn_loaded, 16)
            act.dma_start(w2[:], dram["ffn_w2"].rearrange("(t p) h -> p t h", p=P)).then_inc(ffn_loaded, 16)

            def hi_part(n, dst, src):
                act.wait_ge(job_full, n + 1)
                act.activation(dst, src, ACT.Copy).then_inc(job_hi, 1)

            hi_part(N_A, keep["fold_qk"][:, HI], bank_of(N_A).rearrange("p (t d) -> p t d", t=DT))
            hi_part(N_VO, keep["fold_vo"][:, HI, :, 0:D], bank_of(N_VO).rearrange("p (t d) -> p t d", t=DT))
            for k, (n, kt, g) in enumerate(cross_jobs):
                hi_part(N_CROSS + k, keep["cross_" + n][:, HI, kt, 512 * g:512 * (g + 1)], bank_of(N_CROSS + k))
            for g in range(4):
                n = N_CROSS + 12 + g
                hi_part(n, keep["cross_Wo"][:, HI, 2 * g:2 * g + 2, :], bank_of(n).rearrange("p (t d) -> p t d", t=2))

        @block.tensor
        def _(pe):
            ident = keep["ident"]

            def begin(n):
                if n >= 4:
                    pe.wait_ge(job_done, n - 3)
                return bank_of(n)

            pe.wait_ge(ident_ready, 1)
            pe.wait_ge(attn_loaded, 64)
            for k, n in enumerate(("Wq", "Wk", "Wv")):
                bank = begin(N_T + k)
                for et in range(DT):
                    for dt in range(DT):
                        mm = pe.transpose(bank[:, et * D + dt * P:et * D + (dt + 1) * P],
                                          attn_w[n][:, dt, et * P:(et + 1) * P], ident[:])
                mm.then_inc(job_full, 1)
            for n, left, right in ((N_A, attn_t["Wq"], attn_t["Wk"]), (N_VO, attn_t["Wv"], attn_w["Wo"])):
                bank = begin(n)
                pe.wait_ge(job_done, 3)
                for dt in range(DT):
                    for et in range(DT):
                        mm = pe.matmul(bank[:, dt * D:(dt + 1) * D], left[:, et, dt * P:(dt + 1) * P], right[:, et, :],
                                       start=(et == 0), stop=(et == DT - 1))
                mm.then_inc(job_full, 1)
            bank = begin(N_COL)
            pe.wait_ge(bias_loaded, 16 * 6)
            pe.wait_ge(rows_ready, 2)
            for dt in range(DT):
                for et in range(DT):
                    pe.matmul(bank[:, dt:dt + 1], attn_t["Wq"][:, et, dt * P:(dt + 1) * P], bias["bk"][:, et:et + 1],
                              start=(et == 0), stop=(et == DT - 1))
            for dt in range(DT):
                for et in range(DT):
                    pe.matmul(bank[:, 2 + dt:3 + dt], attn_t["Wk"][:, et, dt * P:(dt + 1) * P], bias["bq"][:, et:et + 1],
                              start=(et == 0), stop=(et == DT - 1))
            for et in range(DT):
                mm = pe.matmul(bank[:, 4:5], bias_rows["bq"][:, et, :], bias["bk"][:, et:et + 1],
                               start=(et == 0), stop=(et == DT - 1))
            mm.then_inc(job_full, 1)
            bank = begin(N_ROW)
            for et in range(DT):
                mm = pe.matmul(bank[:, 0:D], bias_rows["bv"][:, et, :], attn_w["Wo"][:, et, :],
                               start=(et == 0), stop=(et == DT - 1))
            mm.then_inc(job_full, 1)
            pe.wait_ge(cross_loaded, 64)
            for k, (n, kt, g) in enumerate(cross_jobs):
                bank = begin(N_CROSS + k)
                for r in range(4):
                    mm = pe.transpose(bank[:, r * P:(r + 1) * P], cross[n][:, 4 * g + r, kt * P:(kt + 1) * P], ident[:])
                mm.then_inc(job_full, 1)

            def transpose_wide(n, src, g):
                bank = begin(n)
                for t in range(2):
                    for dt in range(DT):
                        et = 2 * g + t
                        mm = pe.transpose(bank[:, t * D + dt * P:t * D + (dt + 1) * P],
                                          src[:, dt, et * P:(et + 1) * P], ident[:])
                mm.then_inc(job_full, 1)

            for g in range(4):
                transpose_wide(N_CROSS + 12 + g, cross_o, g)
            pe.wait_ge(quantised, 1)
            for kt in range(DT):
                for g in range(2):
                    bank = begin(N_FFN + 2 * kt + g)
                    for r in range(4):
                        mm = pe.transpose(bank[:, r * P:(r + 1) * P], w1[:, 4 * g + r, kt * P:(kt + 1) * P], ident[:])
                    mm.then_inc(job_full, 1)
            pe.wait_ge(quantised, 2)
            for g in range(4):
                transpose_wide(N_FFN + 4 + g, w2, g)

        @block.vector
        def _(dve):
            dve.wait_ge(bias_loaded, 16 * 6)
            for n in ("bq", "bv"):
                dve.tensor_copy(bias_rows[n][:], bias[n][:].unsqueeze(2).to_broadcast([P, DT, P])).then_inc(rows_ready, 1)
            dve.memset(keep["fold_vo"][:, :, :, D + 1:FW].bitcast(F32), 0.0)
            dve.memset(keep["third"][:, :, 0:2], 1.0 / 3.0)
            dve.memset(keep["third"][:, :, 2:3], 1.0 / (3.0 * GROUP))
            dve.memset(keep["negs"][:, :, 0:2], -1.0)
            dve.memset(keep["negs"][:, :, 2:3], -1.0 / GROUP)

            def full(n):
                dve.wait_ge(job_full, n + 1)
                return bank_of(n)

            for k, n in enumerate(("Wq", "Wk", "Wv")):
                dve.tensor_copy(attn_t[n][:].rearrange("p t d -> p (t d)"), full(N_T + k)).then_inc(job_done, 1)

            dve.wait_ge(ffn_loaded, 32)
            for k, w in enumerate((w1, w2)):
                dve.tensor_reduce(wabs[:, k:k + 1], w[:].rearrange("p t d -> p (t d)"), AX, ALU.max,
                                  apply_absolute_value=True).then_inc(abs_ready, 1)

            def lo_part(n, dst, src, hi):
                dve.wait_ge(job_hi, hi_count(n))
                dve.tensor_tensor(dst, src, hi.bitcast(F32), ALU.subtract).then_inc(job_done, 1)

            for n, w, m in ((N_A, keep["fold_qk"], D), (N_VO, keep["fold_vo"], D)):
                src = full(n).rearrange("p (t d) -> p t d", t=DT)
                lo_part(n, w[:, LO, :, 0:m], src, w[:, HI, :, 0:m])
            bank = full(N_COL)
            u = bank[:, 0:2].unsqueeze(2)
            dve.tensor_copy(keep["fold_vo"][:, HI, :, D:D + 1], u).then_inc(u_hi, 1)
            dve.tensor_copy(keep["g_bias"][:], bank[:, 2:4])
            dve.tensor_copy(keep["qk_bias"][:], bank[:, 4:5])
            dve.wait_ge(u_hi, 1)
            dve.tensor_tensor(keep["fold_vo"][:, LO, :, D:D + 1], u, keep["fold_vo"][:, HI, :, D:D + 1].bitcast(F32),
                              ALU.subtract).then_inc(job_done, 1)
            bank = full(N_ROW)
            dve.tensor_tensor(keep["bo_row"][:], bank[:, 0:D], keep["bo_row"][:], ALU.add).then_inc(job_done, 1)

            def quantise(k, w):
                dve.wait_ge(abs_all, k + 1)
                dve.tensor_scalar(keep["w_scale"][:, k:k + 1], wmax[:, k:k + 1], MIN_RANGE, 1.0 / QP,
                                  ALU.max, ALU.mult).then_inc(scale_step, 1)
                dve.wait_ge(scale_step, 2 * k + 1)
                dve.reciprocal(winv[:, k:k + 1], keep["w_scale"][:, k:k + 1]).then_inc(scale_step, 1)
                dve.wait_ge(scale_step, 2 * k + 2)
                dve.tensor_scalar(w[:], w[:], winv[:, k:k + 1], MAGIC, ALU.mult, ALU.add).then_inc(quant_step, 1)
                dve.wait_ge(quant_step, k + 1)
                dve.tensor_scalar(w[:], w[:], MAGIC, None, ALU.subtract).then_inc(quantised, 1)

            for k, (n, kt, g) in enumerate(cross_jobs):
                w = keep["cross_" + n]
                lo_part(N_CROSS + k, w[:, LO, kt, 512 * g:512 * (g + 1)], full(N_CROSS + k),
                        w[:, HI, kt, 512 * g:512 * (g + 1)])
                if k == 3:
                    quantise(0, w1)
                if k == 7:
                    quantise(1, w2)
            for g in range(4):
                n = N_CROSS + 12 + g
                w = keep["cross_Wo"]
                lo_part(n, w[:, LO, 2 * g:2 * g + 2, :], full(n).rearrange("p (t d) -> p t d", t=2),
                        w[:, HI, 2 * g:2 * g + 2, :])
            for kt in range(DT):
                for g in range(2):
                    dve.tensor_copy(keep["w1_q"][:, kt, 512 * g:512 * (g + 1)],
                                    full(N_FFN + 2 * kt + g)).then_inc(job_done, 1)
            for g in range(4):
                dve.tensor_copy(keep["w2_q"][:, 2 * g:2 * g + 2, :].rearrange("p t d -> p (t d)"),
                                full(N_FFN + 4 + g)).then_inc(job_done, 1)


def attentions(nc, dram, keep, psum, x2_dram):
    with ExitStack() as ctx:
        def sb(name, shape, dt=F32):
            return ctx.enter_context(nc.sbuf_tensor(name, shape, dt))

        def sem(name):
            return ctx.enter_context(nc.semaphore(name))

        x_in = sb("x_in", [P, 2, D])
        ctx_in = sb("ctx_in", [P, 2, D])
        x_bias = sb("x_bias", [P, 2, D])
        xn = sb("xn", [P, 2, D])
        ctx_t = sb("ctx_t", [P, 2, DT, 2 * P], F32R)
        xn_t = sb("xn_t", [P, 2, DT, 2 * P], F32R)
        g_t = sb("g_t", [P, 2, DT, 2 * P], F32R)
        v_fold = sb("v_fold", [P, 2, 2, D], F32R)
        raw = sb("raw", [P, 2, P])
        left = sb("left", [P, 2, P])
        top8 = sb("top8", [P, 2, 8])
        win_in = sb("win_in", [P, 2, P])
        sparse_in = sb("sparse_in", [P, 2, P])
        comp_in = sb("comp_in", [P, 2, P // GROUP])
        win_e = sb("win_e", [P, 2, P])
        sparse_e = sb("sparse_e", [P, 2, P])
        comp_e = sb("comp_e", [P, 2, P // GROUP])
        maxes = sb("maxes", [P, 2, 3])
        neg_maxes = sb("neg_maxes", [P, 2, 3])
        sums = sb("sums", [P, 2, 3])
        inv_sums = sb("inv_sums", [P, 2, 3])
        weights = sb("weights", [P, 2, 3])
        mix_a = sb("mix_a", [P, 2, P])
        mix_b = sb("mix_b", [P, 2, P])
        probs = sb("probs", [P, 2, P])
        probs_t = sb("probs_t", [P, 2, 2, P], F32R)
        x1 = sb("x1", [P, 2, D])
        x1_old = sb("x1_old", [P, D])
        xn1 = sb("xn1", [P, 2, D])
        xn1_t = sb("xn1_t", [P, 2, DT, 2 * P], F32R)
        row_rq = sb("row_rq", [P, 2])
        stats = sb("stats", [P, 2, 6])
        moments = sb("moments", [P, 2, 2])
        var_eps = sb("var_eps", [P, 2])
        rstd = sb("rstd", [P, 2])
        stats1 = sb("stats1", [P, 2, 6])
        moments1 = sb("moments1", [P, 2, 2])
        var_eps1 = sb("var_eps1", [P, 2])
        rstd1 = sb("rstd1", [P, 2])
        start = sb("start", [P, 10])
        q_t = sb("q_t", [P, 2, ET, 2 * P], F16)
        k_t = sb("k_t", [P, 2, ET, 2 * P], F16)
        q_stack = sb("q_stack", [P, 2, ET, 2 * P], F16)
        k_stack = sb("k_stack", [P, 2, 2, ET, 2 * P], F16)
        v_nat = sb("v_nat", [P, 2, 2, HEADS, VW], F16)
        mask = sb("mask", [P, 2, P])
        scores = sb("scores", [P, 2, QUAD, P])
        score_max = sb("score_max", [P, 2, QUAD])
        neg_max = sb("neg_max", [P, 2, QUAD])
        expd = sb("expd", [P, 2, QUAD, P])
        exp_t = sb("exp_t", [P, 2, 2, QUAD, P], F16)
        inv_den = sb("inv_den", [P, 2, QUAD])
        heads_out = sb("heads_out", [P, 2, 2 * QUAD * DH])
        heads_t = sb("heads_t", [P, 2, ET, P], F32R)
        x2 = sb("x2", [P, 2, D])

        fj_bank = lambda k: psum[:, k % 2, :]
        sc_bank = lambda q: psum[:, 2 + q % 2, :]
        et_bank = lambda q: psum[:, 4 + q % 2, :]
        bj_bank = lambda k: psum[:, 6 + k % 2, :]

        x_loaded, ctx_loaded = sem("x_loaded"), sem("ctx_loaded")
        mask_loaded = [sem("mask_loaded0"), sem("mask_loaded1")]
        q_stacked = [sem(f"q_stacked{n}") for n in range(4)]
        k_stacked = sem("k_stacked")
        x2_free = [sem("x2_free0"), sem("x2_free1")]
        fj_full, fj_hi, fj_free = sem("fj_full"), sem("fj_hi"), sem("fj_free")
        sc_full, sc_free = sem("sc_full"), sem("sc_free")
        et_full, et_hi, et_free = sem("et_full"), sem("et_hi"), sem("et_free")
        bj_full, bj_hi, bj_free = sem("bj_full"), sem("bj_hi"), sem("bj_free")
        stats_x, moments_x, eps_x, rstd_x, xn_ready = (sem(n) for n in ("stats_x", "moments_x", "eps_x", "rstd_x", "xn_ready"))
        stats_x1, moments_x1, eps_x1, rstd_x1, xn1_ready = (sem(n) for n in ("stats_x1", "moments_x1", "eps_x1", "rstd_x1", "xn1_ready"))
        x_bias_ready, x1_kept = sem("x_bias_ready"), sem("x1_kept")
        rq_ready, raw_ready, top_found, top_out = sem("rq_ready"), sem("raw_ready"), sem("top_found"), sem("top_out")
        comp_ready, sparse_ready, max_ready, softmax_in = sem("comp_ready"), sem("sparse_ready"), sem("max_ready"), sem("softmax_in")
        softmax_exp, inv_ready, weights_ready, mix_a_ready, mix_b_ready, probs_ready = (
            sem(n) for n in ("softmax_exp", "inv_ready", "weights_ready", "mix_a_ready", "mix_b_ready", "probs_ready"))
        scores_ready, exp_ready, den_ready = sem("scores_ready"), sem("exp_ready"), sem("den_ready")

        fj = lambda i, k: (i + 1) * FJ + (k + 1)
        fj_his = lambda i, k: (i + 1) * len(WITH_HI) + (WITH_HI.index(k) + 1)
        bj = lambda j, name: j * BJ + (BACK.index(name) + 1)
        bj_his = lambda j, c: j * 4 + (c + 1)
        quad = lambda j, q: j * QUADS + (q + 1)
        hilo = lambda t, *at: (t[(slice(None), HI, *at)], t[(slice(None), LO, *at)])
        tok = lambda b: slice(b * P, (b + 1) * P)
        tile = lambda t: slice(t * P, (t + 1) * P)

        block = ctx.enter_context(nc.Block())

        @block.sync
        def _(sp):
            x_pairs = dram["x"].rearrange("(i b) s d -> i s b d", b=2)
            ctx_pairs = dram["ctx"].rearrange("(i b) s d -> i s b d", b=2)
            mask_rows = dram["mask"].rearrange("(i b) one s k -> i b (one s) k", b=2)
            x2_rows = x2_dram.rearrange("(i b) s d -> i b s d", b=2)

            def stack_queries(i, n):
                wait_apart(sp, fj_free, fj(i, J_Q[n]) + FREE)
                for part in (HI, LO):
                    for parity in range(2):
                        sp.dma_start(q_stack[64 * part:64 * part + 64, parity, 2 * n:2 * n + 2],
                                     q_t[64 * parity:64 * parity + 64, part, 2 * n:2 * n + 2]).then_inc(q_stacked[n], 16)

            def body(i, front, back, ahead):
                j = i - 1
                if back:
                    stack_queries(i, 0)
                    stack_queries(i, 1)
                if ahead:
                    wait_apart(sp, xn_ready, i + 1)
                    wait_apart(sp, x_bias_ready, i + 1)
                    sp.dma_start(x_in[:], x_pairs[i + 1]).then_inc(x_loaded, 16)
                    wait_apart(sp, fj_full, fj(i, J_CTX))
                    sp.dma_start(ctx_in[:], ctx_pairs[i + 1]).then_inc(ctx_loaded, 16)
                if back:
                    for n in range(2, 4):
                        stack_queries(i, n)
                    if front:
                        wait_apart(sp, sc_free, quad(j, 3) + FREE)
                        sp.dma_start(mask[:, 0, :], mask_rows[i, 0]).then_inc(mask_loaded[0], 16)
                if front:
                    wait_apart(sp, fj_free, fj(i, J_K3) + FREE)
                    if back:
                        wait_apart(sp, sc_full, quad(j, 7))
                    for part in (HI, LO):
                        for parity in range(2):
                            for half in range(2):
                                sp.dma_start(k_stack[64 * half:64 * half + 64, part, parity],
                                             k_t[64 * parity:64 * parity + 64, part]).then_inc(k_stacked, 16)
                if back:
                    wait_apart(sp, bj_free, bj(j, "out0") + FREE)
                    sp.dma_start(x2_rows[j, 0], x2[:, 0, :]).then_inc(x2_free[0], 16)
                    if front:
                        wait_apart(sp, sc_free, quad(j, 7) + FREE)
                        sp.dma_start(mask[:, 1, :], mask_rows[i, 1]).then_inc(mask_loaded[1], 16)
                    wait_apart(sp, bj_free, bj(j, "out1") + FREE)
                    sp.dma_start(x2_rows[j, 1], x2[:, 1, :]).then_inc(x2_free[1], 16)

            sp.dma_start(x_in[:], x_pairs[0]).then_inc(x_loaded, 16)
            sp.dma_start(ctx_in[:], ctx_pairs[0]).then_inc(ctx_loaded, 16)
            for b in range(2):
                sp.dma_start(mask[:, b, :], mask_rows[0, b]).then_inc(mask_loaded[b], 16)
            body(0, True, False, True)
            with sp.Fori(1, PAIRS - 1) as i:
                body(i, True, True, True)
            body(PAIRS - 1, True, True, False)
            body(PAIRS, False, True, False)
            for b in range(2):
                wait_apart(sp, x2_free[b], 16 * (PAIRS + 1))

        @block.gpsimd
        def _(pool):
            def reciprocal_deviation(i, moments_done, mom, ve, eps_done, out, done):
                wait_apart(pool, moments_done, i + 1)
                pool.tensor_scalar(ve[:], mom[:, :, 1], EPS, None, ALU.add).then_inc(eps_done, 1)
                pool.wait_ge(eps_done, i + 1)
                pool.tensor_tensor(out[:], ve[:], keep["half"], ALU.pow).then_inc(done, 1)

            def body(i, front, back, ahead):
                if back:
                    wait_apart(pool, bj_free, bj(i - 2, "out1") + FREE)
                    wait_apart(pool, fj_free, fj(i - 1, J_AO) + FREE)
                    pool.tensor_copy(x1_old[:], x1[:, 1, :]).then_inc(x1_kept, 1)
                if front:
                    if not back:
                        pool.wait_ge(x_loaded, 16 * (i + 1))
                    for b in range(2):
                        op = pool.tensor_tensor(x_bias[:, b, :], x_in[:, b, :], keep["bo_row"][:], ALU.add)
                    op.then_inc(x_bias_ready, 1)
                if ahead:
                    reciprocal_deviation(i + 1, moments_x, moments, var_eps, eps_x, rstd, rstd_x)
                if front:
                    reciprocal_deviation(i, moments_x1, moments1, var_eps1, eps_x1, rstd1, rstd_x1)

            body(-1, False, False, True)
            body(0, True, False, True)
            with pool.Fori(1, PAIRS - 1) as i:
                body(i, True, True, True)
            body(PAIRS - 1, True, True, False)
            body(PAIRS, False, True, False)

        @block.tensor
        def _(pe):
            ident = keep["ident"][:]

            def body(i, front, back, ahead):
                j = i - 1

                def begin(k):
                    pe.wait_ge(fj_free, fj(i, k) - max(0, left_out(k, range(FJ), front, back, ahead) - 1))
                    return fj_bank(k)

                def done(mm, k):
                    mm.then_inc(fj_full, steps(k, range(FJ), front, back, ahead))

                def evacuated(k):
                    pe.wait_ge(fj_free, fj(i, k) + FREE)

                def transpose_pair(k, src):
                    bank = begin(k)
                    for dt in range(DT):
                        for b in range(2):
                            mm = pe.transpose(bank[:, tile(2 * dt + b)], src[:, b, tile(dt)], ident)
                    done(mm, k)

                def project(k, out_tiles, w, src):
                    bank = begin(k)
                    for m, mt in enumerate(out_tiles):
                        for kt in range(DT):
                            mm = split_products(pe, bank[:, m * 2 * P:(m + 1) * 2 * P], hilo(w, kt, tile(mt)),
                                                hilo(src, kt), first=(kt == 0), last=(kt == DT - 1))
                    done(mm, k)

                def context_transpose():
                    pe.wait_ge(ctx_loaded, 16 * (i + 1))
                    transpose_pair(J_CTX, ctx_in)

                def x_transpose():
                    pe.wait_ge(xn_ready, i + 2)
                    transpose_pair(J_X, xn)

                def fold_query():
                    evacuated(J_X)
                    project(J_G, range(DT), keep["fold_qk"], xn_t)

                def fold_value(b):
                    bank = begin(J_V0 if b == 0 else J_V1)
                    for kt in range(DT):
                        mm = split_products(pe, bank[:, 0:FW], hilo(xn_t, kt, tok(b)), hilo(keep["fold_vo"], kt),
                                            first=(kt == 0), last=(kt == DT - 1))
                    done(mm, J_V0 if b == 0 else J_V1)

                def raw_scores():
                    evacuated(J_G)
                    bank = begin(J_RAW)
                    for b in range(2):
                        for kt in range(DT):
                            mm = split_products(pe, bank[:, b * 2 * P:(b + 1) * 2 * P], hilo(g_t, kt, tok(b)),
                                                hilo(xn_t, kt), first=(kt == 0), last=(kt == DT - 1))
                    done(mm, J_RAW)

                def keys(n):
                    project(J_K[n], (2 * n, 2 * n + 1), keep["cross_Wk"], ctx_t)

                def values(n):
                    k, b, half = J_VV[n], n // 2, n % 2
                    bank = begin(k)
                    for kt in range(DT):
                        mm = split_products(pe, bank, hilo(ctx_t, kt, tok(b)),
                                            hilo(keep["cross_Wv"], kt, slice(half * 512, half * 512 + 512)),
                                            first=(kt == 0), last=(kt == DT - 1))
                    done(mm, k)

                def probs_transpose(b):
                    pe.wait_ge(probs_ready, i * 2 + (b + 1))
                    bank = begin(J_PT0 + b)
                    done(pe.transpose(bank[:, 0:P], probs[:, b, :], ident), J_PT0 + b)

                def attend():
                    evacuated(J_PT1)
                    bank = begin(J_AO)
                    for b in range(2):
                        mm = split_products(pe, bank[:, b * D:(b + 1) * D], hilo(probs_t, b), hilo(v_fold, b))
                    done(mm, J_AO)

                def x1_transpose():
                    pe.wait_ge(xn1_ready, i)
                    transpose_pair(J_X1, xn1)

                def queries(n):
                    if n == 0:
                        evacuated(J_X1)
                    project(J_Q[n], (2 * n, 2 * n + 1), keep["cross_Wq"], xn1_t)

                def score(q):
                    if q == 0:
                        pe.wait_ge(k_stacked, j * 128 + 128)
                    if q < 4:
                        pe.wait_ge(q_stacked[q], i * 64 + 64)
                    b, t0 = q // QUAD, 2 * (q % QUAD)
                    pe.wait_ge(sc_free, quad(j, q))
                    bank = sc_bank(q)
                    for h in range(QUAD):
                        t, parity = t0 + h // 2, h % 2
                        for part in (HI, LO):
                            mm = pe.matmul(bank[:, tile(h)], q_stack[:, parity, t, tok(b)],
                                           k_stack[:, part, parity, t, tok(b)], start=(part == HI), stop=(part == LO))
                    mm.then_inc(sc_full, 1)

                def exp_transpose(q):
                    pe.wait_ge(exp_ready, quad(j, q))
                    pe.wait_ge(et_free, quad(j, q))
                    for h in range(QUAD):
                        mm = pe.transpose(et_bank(q)[:, tile(h)], expd[:, q % 2, h, :], ident)
                    mm.then_inc(et_full, 1)

                def back_begin(name):
                    k = BACK.index(name)
                    pe.wait_ge(bj_free, bj(j, name))
                    return bj_bank(k)

                def weigh(q):
                    b = q // QUAD
                    pe.wait_ge(et_free, quad(j, q) + FREE)
                    pe.wait_ge(fj_free, fj(j, (J_VV1, J_VV3)[b]) + FREE)
                    bank = back_begin(f"pv{q}")
                    for h in range(QUAD):
                        head = QUAD * (q % QUAD) + h
                        mm = split_products(pe, bank[:, h * VW:(h + 1) * VW], hilo(exp_t[:, q % 2], h),
                                            hilo(v_nat, b, head))
                    mm.then_inc(bj_full, 1)

                def heads_transpose(c):
                    pe.wait_ge(bj_free, bj(j, f"pv{2 * c + 1}") + FREE)
                    bank = back_begin(f"ct{c}")
                    for t in range(4):
                        mm = pe.transpose(bank[:, tile(t)], heads_out[:, c % 2, tile(t)], ident)
                    mm.then_inc(bj_full, 1)

                def output(b):
                    pe.wait_ge(bj_free, bj(j, f"ct{2 * b + 1}") + FREE)
                    bank = back_begin(f"out{b}")
                    for kt in range(ET):
                        mm = split_products(pe, bank[:, 0:D], hilo(heads_t, kt), hilo(keep["cross_Wo"], kt),
                                            first=(kt == 0), last=(kt == ET - 1))
                    mm.then_inc(bj_full, 1)

                if back:
                    x1_transpose()
                if front:
                    context_transpose()
                if back:
                    queries(0)
                if front:
                    keys(0)
                if back:
                    queries(1)
                if front:
                    keys(1)
                if back:
                    score(0)
                    queries(2)
                    score(1)
                    queries(3)
                    score(2)
                    exp_transpose(0)
                if front:
                    keys(2)
                if back:
                    score(3)
                    exp_transpose(1)
                    weigh(0)
                if front:
                    keys(3)
                if back:
                    score(4)
                    exp_transpose(2)
                    weigh(1)
                    score(5)
                    exp_transpose(3)
                    weigh(2)
                if ahead:
                    x_transpose()
                if back:
                    heads_transpose(0)
                    score(6)
                    exp_transpose(4)
                    weigh(3)
                if ahead:
                    fold_query()
                if back:
                    heads_transpose(1)
                    score(7)
                if front:
                    values(0)
                if back:
                    exp_transpose(5)
                    weigh(4)
                if front:
                    values(1)
                    probs_transpose(0)
                    probs_transpose(1)
                if back:
                    exp_transpose(6)
                    weigh(5)
                    output(0)
                if front:
                    attend()
                if back:
                    exp_transpose(7)
                    weigh(6)
                if ahead:
                    fold_value(0)
                if back:
                    heads_transpose(2)
                if ahead:
                    fold_value(1)
                if back:
                    weigh(7)
                if front:
                    values(2)
                if ahead:
                    raw_scores()
                if back:
                    heads_transpose(3)
                if front:
                    values(3)
                if back:
                    output(1)

            body(-1, False, False, True)
            body(0, True, False, True)
            with pe.Fori(1, PAIRS - 1) as i:
                body(i, True, True, True)
            body(PAIRS - 1, True, True, False)
            body(PAIRS, False, True, False)

        def landing(k):
            bank = fj_bank(k)
            pair = bank.rearrange("p (t s) -> p t s", t=2)
            if k == J_CTX:
                return ctx_t, (), pair
            if k == J_X:
                return xn_t, (), pair
            if k == J_X1:
                return xn1_t, (), pair
            if k in (J_V0, J_V1):
                return v_fold, (int(k == J_V1),), bank[:, 0:D]
            if k in J_K or k in J_Q:
                n = (J_K if k in J_K else J_Q).index(k)
                return (k_t if k in J_K else q_t), (slice(2 * n, 2 * n + 2),), pair
            if k in (J_PT0, J_PT1):
                return probs_t, (k - J_PT0,), bank[:, 0:P]
            n = J_VV.index(k)
            half = HEADS // 2
            return (v_nat, (n // 2, slice(half * (n % 2), half * (n % 2) + half), slice(0, DH)),
                    bank.rearrange("p (h d) -> p h d", d=DH))

        @block.scalar
        def _(act):
            def body(i, front, back, ahead):
                j = i - 1

                def hi(k):
                    act.wait_ge(fj_full, fj(i, k))
                    if k == J_K0 and back:
                        act.wait_ge(k_stacked, i * 128)
                    if k in J_Q:
                        act.wait_ge(q_stacked[J_Q.index(k)], i * 64)
                    if k == J_G:
                        for t in range(DT):
                            op = act.activation(g_t[:, HI, t, :], fj_bank(k)[:, t * 2 * P:(t + 1) * 2 * P],
                                                ACT.Identity, bias=keep["g_bias"][:, t:t + 1])
                    else:
                        dst, at, src = landing(k)
                        op = act.activation(hilo(dst, *at)[HI], src, ACT.Copy)
                    op.then_inc(fj_hi, steps(k, WITH_HI, front, back, ahead))

                def exponential(q):
                    act.wait_ge(scores_ready, quad(j, q))
                    for h in range(QUAD):
                        op = act.activation(expd[:, q % 2, h, :], scores[:, q % 2, h, :], ACT.Exp,
                                            bias=neg_max[:, q % 2, h:h + 1])
                    op.then_inc(exp_ready, 1)

                def exp_hi(q):
                    act.wait_ge(et_full, quad(j, q))
                    act.activation(exp_t[:, q % 2, HI], et_bank(q).rearrange("p (h s) -> p h s", h=QUAD),
                                   ACT.Copy).then_inc(et_hi, 1)

                def heads_hi(c):
                    act.wait_ge(bj_full, bj(j, f"ct{c}"))
                    act.activation(heads_t[:, HI, 4 * (c % 2):4 * (c % 2) + 4, :],
                                   bj_bank(BACK.index(f"ct{c}")).rearrange("p (t s) -> p t s", t=4),
                                   ACT.Copy).then_inc(bj_hi, 1)

                def self_softmax():
                    act.wait_ge(softmax_in, i + 1)
                    for b in range(2):
                        for k, (src, dst, scale) in enumerate(((win_in, win_e, 1.0), (sparse_in, sparse_e, 1.0),
                                                               (comp_in, comp_e, 1.0 / GROUP))):
                            op = act.activation(dst[:, b, :], src[:, b, :], ACT.Exp, bias=neg_maxes[:, b, k:k + 1],
                                                scale=scale, accum_out=sums[:, b, k:k + 1])
                    op.then_inc(softmax_exp, 1)

                if back:
                    hi(J_X1)
                if front:
                    hi(J_CTX)
                if back:
                    hi(J_Q0)
                if front:
                    hi(J_K0)
                if back:
                    hi(J_Q1)
                if front:
                    hi(J_K1)
                if back:
                    exponential(0)
                    hi(J_Q2)
                    exponential(1)
                    hi(J_Q3)
                    exp_hi(0)
                    exponential(2)
                if front:
                    hi(J_K2)
                if back:
                    exp_hi(1)
                    exponential(3)
                if front:
                    hi(J_K3)
                if back:
                    exp_hi(2)
                    exponential(4)
                if front:
                    self_softmax()
                if back:
                    exp_hi(3)
                    exponential(5)
                if ahead:
                    hi(J_X)
                if back:
                    heads_hi(0)
                    exp_hi(4)
                    exponential(6)
                if ahead:
                    hi(J_G)
                if back:
                    heads_hi(1)
                if front:
                    hi(J_VV0)
                if back:
                    exp_hi(5)
                    exponential(7)
                if front:
                    hi(J_VV1)
                    hi(J_PT0)
                    hi(J_PT1)
                if back:
                    exp_hi(6)
                    exp_hi(7)
                if ahead:
                    hi(J_V0)
                if back:
                    heads_hi(2)
                if ahead:
                    hi(J_V1)
                if front:
                    hi(J_VV2)
                if back:
                    heads_hi(3)
                if front:
                    hi(J_VV3)

            body(-1, False, False, True)
            body(0, True, False, True)
            with act.Fori(1, PAIRS - 1) as i:
                body(i, True, True, True)
            body(PAIRS - 1, True, True, False)
            body(PAIRS, False, True, False)

        @block.vector
        def _(dve):
            dve.memset(v_nat[:, HI, :, :, DH:DH + 1], 1.0)
            dve.memset(v_nat[:, HI, :, :, DH + 1:VW], 0.0)
            dve.memset(v_nat[:, LO, :, :, DH:VW], 0.0)
            dve.memset(start[:, 0:1], 0.0).then_inc(fj_free, FREE)
            dve.memset(start[:, 1:2], 0.0).then_inc(sc_free, FREE)
            dve.memset(start[:, 2:3], 0.0).then_inc(et_free, FREE)
            dve.memset(start[:, 3:4], 0.0).then_inc(bj_free, FREE)
            for b in range(2):
                dve.memset(start[:, 4 + b:5 + b], 0.0).then_inc(x2_free[b], 16)
            for n in range(4):
                dve.memset(start[:, 6 + n:7 + n], 0.0).then_inc(q_stacked[n], 64)

            def body(i, front, back, ahead):
                j = i - 1

                def lo(k):
                    dve.wait_ge(fj_hi, fj_his(i, k))
                    if k == J_G:
                        for t in range(DT):
                            op = dve.scalar_tensor_tensor(g_t[:, LO, t, :], fj_bank(k)[:, t * 2 * P:(t + 1) * 2 * P],
                                                          keep["g_bias"][:, t:t + 1], g_t[:, HI, t, :].bitcast(F32),
                                                          ALU.add, ALU.subtract)
                    else:
                        dst, at, src = landing(k)
                        hi = hilo(dst, *at)[HI]
                        hi = hi.bitcast(F32) if dst.dtype == F32R else hi
                        if k in (J_V0, J_V1):
                            b = int(k == J_V1)
                            dve.tensor_scalar(row_rq[:, b:b + 1], fj_bank(k)[:, D:D + 1],
                                              keep["qk_bias"][:], None, ALU.add).then_inc(rq_ready, 1)
                        op = dve.tensor_tensor(hilo(dst, *at)[LO], src, hi, ALU.subtract)
                    op.then_inc(fj_free, steps(k, range(FJ), front, back, ahead))

                def statistics(n, src, st, stats_done, mom, moments_done):
                    if src is x1:
                        wait_apart(dve, fj_free, fj(n, J_AO) + FREE)
                    for b in range(2):
                        op = dve.bn_stats(st[:, b, :], src[:, b, :])
                    op.then_inc(stats_done, 1)
                    wait_apart(dve, stats_done, n + 1)
                    for b in range(2):
                        op = dve.bn_aggr(mom[:, b, :], st[:, b, :])
                    op.then_inc(moments_done, 1)

                def normalise(n, src, mom, rs, rstd_done, dst, done):
                    dve.wait_ge(rstd_done, n + 1)
                    for b in range(2):
                        op = dve.tensor_scalar(dst[:, b, :], src[:, b, :], mom[:, b, 0:1], rs[:, b:b + 1],
                                               ALU.subtract, ALU.mult)
                    op.then_inc(done, 1)

                def add_mask(q):
                    b = q // QUAD
                    if q % QUAD == 0:
                        wait_apart(dve, mask_loaded[b], 16 * (j + 1))
                    if q >= 2:
                        wait_apart(dve, exp_ready, quad(j, q - 2))
                    wait_apart(dve, sc_full, quad(j, q))
                    for h in range(QUAD):
                        op = dve.tensor_tensor_reduce(scores[:, q % 2, h, :], sc_bank(q)[:, tile(h)], mask[:, b, :],
                                                      1.0, NEG, ALU.add, ALU.max, score_max[:, q % 2, h:h + 1])
                    op.then_inc(sc_free, 1)

                def negate_max(q):
                    dve.wait_ge(sc_free, quad(j, q) + FREE)
                    dve.tensor_scalar(neg_max[:, q % 2, :], score_max[:, q % 2, :], -1.0, None,
                                      ALU.mult).then_inc(scores_ready, 1)

                def mask_scores(q):
                    add_mask(q)
                    negate_max(q)

                def exp_lo(q):
                    dve.wait_ge(et_hi, quad(j, q))
                    dve.tensor_tensor(exp_t[:, q % 2, LO], et_bank(q).rearrange("p (h s) -> p h s", h=QUAD),
                                      exp_t[:, q % 2, HI], ALU.subtract).then_inc(et_free, 1)

                def pv_view(q):
                    return bj_bank(BACK.index(f"pv{q}"))[:, 0:QUAD * VW].rearrange("p (h w) -> p h w", w=VW)

                def row_sums(q):
                    dve.wait_ge(bj_full, bj(j, f"pv{q}"))
                    dve.reciprocal(inv_den[:, q % 2, :], pv_view(q)[:, :, DH]).then_inc(den_ready, 1)

                def divide(q):
                    dve.wait_ge(den_ready, quad(j, q))
                    at = slice((q % 2) * QUAD * DH, (q % 2 + 1) * QUAD * DH)
                    dve.tensor_tensor(heads_out[:, (q // 2) % 2, at].rearrange("p (h d) -> p h d", d=DH),
                                      pv_view(q)[:, :, 0:DH], inv_den[:, q % 2, :].unsqueeze(2).to_broadcast([P, QUAD, DH]),
                                      ALU.mult).then_inc(bj_free, 1)

                def heads_lo(c):
                    dve.wait_ge(bj_hi, bj_his(j, c))
                    at = slice(4 * (c % 2), 4 * (c % 2) + 4)
                    dve.tensor_tensor(heads_t[:, LO, at, :], bj_bank(BACK.index(f"ct{c}")).rearrange("p (t s) -> p t s", t=4),
                                      heads_t[:, HI, at, :].bitcast(F32), ALU.subtract).then_inc(bj_free, 1)

                def raw_scores():
                    dve.wait_ge(rq_ready, i * 2 + 4)
                    dve.wait_ge(fj_full, fj(i, J_RAW))
                    for b in range(2):
                        at = b * 2 * P + b * P
                        op = dve.tensor_scalar(raw[:, b, :], fj_bank(J_RAW)[:, at:at + P], row_rq[:, b:b + 1],
                                               1.0 / 16.0, ALU.add, ALU.mult)
                    op.then_inc(fj_free, steps(J_RAW, range(FJ), front, back, ahead))

                def top_round(r):
                    for b in range(2):
                        if r == 0:
                            wait_apart(dve, fj_free, fj(i - 1, J_RAW) + FREE)
                        else:
                            wait_apart(dve, top_out, i * 16 + (2 * (r - 1) + b + 1))
                        dve.max(top8[:, b, :], (raw if r == 0 else left)[:, b, :]).then_inc(top_found, 1)
                    for b in range(2):
                        wait_apart(dve, top_found, i * 16 + (2 * r + b + 1))
                        dve.match_replace(left[:, b, :], top8[:, b, :], (raw if r == 0 else left)[:, b, :],
                                          NEG).then_inc(top_out, 1)

                def window_and_compressed():
                    wait_apart(dve, fj_free, fj(i - 1, J_RAW) + FREE)
                    for b in range(2):
                        dve.tensor_tensor_reduce(win_in[:, b, :], raw[:, b, :], keep["causal"][:], 1.0, NEG,
                                                 ALU.add, ALU.max, maxes[:, b, 0:1])
                    dve.tensor_reduce(comp_in[:], raw[:].rearrange("p b (g f) -> p b g f", f=GROUP), AX,
                                      ALU.add).then_inc(comp_ready, 1)
                    dve.wait_ge(comp_ready, i + 1)
                    dve.tensor_reduce(maxes[:, :, 2], comp_in[:], AX, ALU.max)

                def sparse():
                    dve.wait_ge(top_out, i * 16 + 16)
                    dve.scalar_tensor_tensor(sparse_in[:], left[:], NEG, raw[:], ALU.is_equal,
                                             ALU.mult).then_inc(sparse_ready, 1)
                    dve.wait_ge(sparse_ready, i + 1)
                    dve.tensor_reduce(maxes[:, :, 1], sparse_in[:], AX, ALU.max).then_inc(max_ready, 1)
                    dve.wait_ge(max_ready, i + 1)
                    dve.tensor_tensor(neg_maxes[:], maxes[:], keep["negs"][:], ALU.mult).then_inc(softmax_in, 1)

                def mix():
                    dve.wait_ge(softmax_exp, i + 1)
                    dve.reciprocal(inv_sums[:], sums[:]).then_inc(inv_ready, 1)
                    dve.wait_ge(inv_ready, i + 1)
                    dve.tensor_tensor(weights[:], inv_sums[:], keep["third"][:], ALU.mult).then_inc(weights_ready, 1)
                    dve.wait_ge(weights_ready, i + 1)
                    for b in range(2):
                        dve.tensor_scalar(mix_a[:, b, :], win_e[:, b, :], weights[:, b, 0:1], None,
                                          ALU.mult).then_inc(mix_a_ready, 1)
                    for b in range(2):
                        dve.wait_ge(mix_a_ready, i * 2 + (b + 1))
                        dve.scalar_tensor_tensor(mix_b[:, b, :], sparse_e[:, b, :], weights[:, b, 1:2], mix_a[:, b, :],
                                                 ALU.mult, ALU.add).then_inc(mix_b_ready, 1)
                    for b in range(2):
                        dve.wait_ge(mix_b_ready, i * 2 + (b + 1))
                        dve.scalar_tensor_tensor(probs[:, b, :].rearrange("p (g f) -> p g f", f=GROUP),
                                                 comp_e[:, b, :].unsqueeze(2).to_broadcast([P, P // GROUP, GROUP]),
                                                 weights[:, b, 2:3], mix_b[:, b, :].rearrange("p (g f) -> p g f", f=GROUP),
                                                 ALU.mult, ALU.add).then_inc(probs_ready, 1)

                def first_residual():
                    dve.wait_ge(x_bias_ready, i + 1)
                    if back:
                        dve.wait_ge(x1_kept, i)
                        dve.wait_ge(bj_free, bj(j, "out0") + FREE)
                    dve.wait_ge(fj_full, fj(i, J_AO))
                    dve.tensor_tensor(x1[:].rearrange("p b d -> p (b d)"), fj_bank(J_AO),
                                      x_bias[:].rearrange("p b d -> p (b d)"), ALU.add).then_inc(fj_free, steps(J_AO, range(FJ), front, back, ahead))

                def second_residual(b):
                    dve.wait_ge(bj_full, bj(j, f"out{b}"))
                    dve.wait_ge(x2_free[b], 16 * (j + 1))
                    if b == 1:
                        dve.wait_ge(x1_kept, j + 1)
                    dve.tensor_tensor(x2[:, b, :], bj_bank(BACK.index(f"out{b}"))[:, 0:D],
                                      x1[:, 0, :] if b == 0 else x1_old[:], ALU.add).then_inc(bj_free, 1)

                if back:
                    lo(J_X1)
                if front:
                    top_round(0)
                    lo(J_CTX)
                    top_round(1)
                if back:
                    lo(J_Q0)
                if front:
                    window_and_compressed()
                    lo(J_K0)
                    top_round(2)
                if back:
                    lo(J_Q1)
                if front:
                    top_round(3)
                    lo(J_K1)
                if back:
                    mask_scores(0)
                if front:
                    top_round(4)
                if back:
                    lo(J_Q2)
                    mask_scores(1)
                if front:
                    top_round(5)
                if back:
                    lo(J_Q3)
                    mask_scores(2)
                if front:
                    top_round(6)
                if back:
                    exp_lo(0)
                if front:
                    lo(J_K2)
                if back:
                    mask_scores(3)
                    row_sums(0)
                if front:
                    top_round(7)
                if back:
                    divide(0)
                    exp_lo(1)
                if front:
                    lo(J_K3)
                if back:
                    mask_scores(4)
                    row_sums(1)
                if front:
                    sparse()
                if back:
                    divide(1)
                    exp_lo(2)
                if ahead:
                    dve.wait_ge(x_loaded, 16 * (i + 2))
                    statistics(i + 1, x_in, stats, stats_x, moments, moments_x)
                if back:
                    mask_scores(5)
                    row_sums(2)
                if ahead:
                    normalise(i + 1, x_in, moments, rstd, rstd_x, xn, xn_ready)
                if back:
                    divide(2)
                    exp_lo(3)
                if front:
                    mix()
                if ahead:
                    lo(J_X)
                if back:
                    mask_scores(6)
                    row_sums(3)
                    heads_lo(0)
                    divide(3)
                    exp_lo(4)
                if ahead:
                    lo(J_G)
                if back:
                    mask_scores(7)
                    heads_lo(1)
                if front:
                    lo(J_VV0)
                if back:
                    row_sums(4)
                    exp_lo(5)
                    divide(4)
                if front:
                    lo(J_VV1)
                    lo(J_PT0)
                    lo(J_PT1)
                if back:
                    row_sums(5)
                    exp_lo(6)
                    divide(5)
                    second_residual(0)
                if front:
                    first_residual()
                if back:
                    row_sums(6)
                if front:
                    statistics(i, x1, stats1, stats_x1, moments1, moments_x1)
                if back:
                    divide(6)
                    exp_lo(7)
                if ahead:
                    lo(J_V0)
                if back:
                    heads_lo(2)
                if ahead:
                    lo(J_V1)
                if back:
                    row_sums(7)
                if front:
                    normalise(i, x1, moments1, rstd1, rstd_x1, xn1, xn1_ready)
                if back:
                    divide(7)
                if front:
                    lo(J_VV2)
                if ahead:
                    raw_scores()
                if back:
                    heads_lo(3)
                if front:
                    lo(J_VV3)
                if back:
                    second_residual(1)

            body(-1, False, False, True)
            body(0, True, False, True)
            with dve.Fori(1, PAIRS - 1) as i:
                body(i, True, True, True)
            body(PAIRS - 1, True, True, False)
            body(PAIRS, False, True, False)


def feed_forward(nc, keep, psum, x2_dram, out_dram):
    with ExitStack() as ctx:
        def sb(name, shape, dt=F32):
            return ctx.enter_context(nc.sbuf_tensor(name, shape, dt))

        def sem(name):
            return ctx.enter_context(nc.semaphore(name))

        GB = 4
        GROUPS = NB // GB
        TOK = GB * P
        LAG = 3
        LOAD = 4

        normed = sb("normed", [P, NB, D])
        xq_t = sb("xq_t", [P, DT, NB * P], BF16)
        x_load = sb("x_load", [P, LOAD, D])
        stats = sb("f_stats", [P, LOAD, 6])
        moments = sb("f_moments", [P, LOAD, 2])
        var_eps = sb("f_var_eps", [P, LOAD])
        rstd = sb("f_rstd", [P, LOAD])
        row_max = sb("row_max", [P, NB])
        tile_max = sb("tile_max", [P, GROUPS * ET])
        peak = sb("peak", [P, 4])
        scale = sb("act_scale", [P, 2])
        inv_scale = sb("inv_scale", [P, 2])
        both = sb("both_scales", [P, 2])
        b1_scaled = sb("b1_scaled", [P, ET])
        b2_scaled = sb("b2_scaled", [P, D])
        rounded = sb("rounded", [P, GB, D])
        xq = sb("xq", [P, GB, D], BF16)
        start = sb("f_start", [P, 6])
        ident16 = sb("ident16", [P, P], BF16)
        hidden = sb("hidden", [P, 2, TOK])
        h_round = sb("h_round", [P, 2, TOK])
        h_q = sb("h_q", [P, 4, TOK], BF16)
        x_again = sb("x_again", [P, 2, GB, D])
        result = sb("result", [P, GB, D])

        loaded, moments_done, stats_done, eps_done, rstd_done, max_done = (
            sem(n) for n in ("f_loaded", "f_moments_done", "f_stats_done", "f_eps_done", "f_rstd_done", "f_max_done"))
        norm_done = sem("f_norm_done")
        peak_own, peak_all, scale_step, scales_done = sem("peak_own"), sem("peak_all"), sem("f_scale_step"), sem("scales_done")
        xq_rounded, xq_ready, xt_full, xt_done = sem("xq_rounded"), sem("xq_ready"), sem("xt_full"), sem("xt_done")
        ident_done = sem("ident_done")
        u_full, h_ready, h_seen = sem("u_full"), sem("h_ready"), sem("h_seen")
        u2_full, h2_ready, h2_rounded, hq_ready = sem("u2_full"), sem("h2_ready"), sem("h2_rounded"), sem("hq_ready")
        acc_step, acc_full, acc_free = sem("acc_step"), sem("acc_full"), sem("acc_free")
        again_loaded = [sem("again_loaded0"), sem("again_loaded1")]
        bias_added, stored = sem("bias_added"), sem("stored")

        x2_groups = x2_dram.rearrange("(g b) s d -> g s b d", b=GB)
        out_groups = out_dram.rearrange("(g b) s d -> g s b d", b=GB)
        u_bank = lambda t: psum[:, t % 4, :]
        xt_bank = psum[:, 4, :].bitcast(BF16)

        block = ctx.enter_context(nc.Block())

        @block.sync
        def _(sp):
            def load(g):
                sp.dma_start(x_load[:], x2_groups[g]).then_inc(loaded, 16)

            load(0)
            with sp.Fori(1, GROUPS) as g:
                wait_apart(sp, norm_done, g)
                load(g)
            def reload(n, side):
                sp.dma_start(x_again[:, side], x2_groups[n]).then_inc(again_loaded[side], 16)

            reload(0, 0)
            reload(1, 1)

            def store(n):
                wait_apart(sp, acc_free, GB * (n + 2))
                sp.dma_start(out_groups[n], result[:]).then_inc(stored, 16)

            with sp.Fori(0, GROUPS // 2 - 1) as h:
                for side in range(2):
                    store(h * 2 + side)
                    reload(h * 2 + side + 2, side)
            store(GROUPS - 2)
            store(GROUPS - 1)
            wait_apart(sp, stored, 16 * (GROUPS + 1))

        @block.gpsimd
        def _(pool):
            with pool.Fori(0, GROUPS) as g:
                wait_apart(pool, moments_done, g + 1)
                pool.tensor_scalar(var_eps[:], moments[:, :, 1], EPS, None, ALU.add).then_inc(eps_done, 1)
                pool.wait_ge(eps_done, g + 1)
                pool.tensor_tensor(rstd[:], var_eps[:], keep["half4"][:], ALU.pow).then_inc(rstd_done, 1)
            for k in range(2):
                pool.wait_ge(peak_own, k + 1)
                pool.partition_all_reduce(peak[:, 2 * k + 1:2 * k + 2], peak[:, 2 * k:2 * k + 1], P,
                                          RMAX).then_inc(peak_all, 1)

            pool.wait_ge(scales_done, 2)
            with pool.Fori(0, GROUPS // 2) as h:
                for side in range(2):
                    pool.wait_ge(again_loaded[side], h * 16 + 16)
                    for b in range(GB):
                        op = pool.tensor_tensor(x_again[:, side, b, :], x_again[:, side, b, :], b2_scaled[:], ALU.add)
                    op.then_inc(bias_added, 1)

        def hidden_tile(pe, g, t, full, ready):
            for kt in range(DT):
                mm = pe.matmul(u_bank(t), keep["w1_q"][:, kt, t * P:(t + 1) * P], xq_t[:, kt, bass.ts(g, TOK)],
                               start=(kt == 0), stop=(kt == DT - 1))
            mm.then_inc(full, 1)

        @block.tensor
        def _(pe):
            with pe.Fori(0, GROUPS) as g:
                pe.wait_ge(xq_ready, g + 1)
                pe.wait_ge(ident_done, 1)
                for dt in range(DT):
                    for b in range(GB):
                        mm = pe.transpose(xt_bank[:, (dt * GB + b) * P:(dt * GB + b + 1) * P],
                                          xq[:, b, dt * P:(dt + 1) * P], ident16[:])
                mm.then_inc(xt_full, 1)
                pe.wait_ge(xt_done, g + 1)
                for t in range(ET):
                    pe.wait_ge(h_ready, g * ET + (t + 1))
                    hidden_tile(pe, g, t, u_full, None)

            def second_layer(n_tile, t, first, last):
                pe.wait_ge(hq_ready, n_tile)
                for b in range(GB):
                    mm = pe.matmul(psum[:, 4 + b, 0:D], h_q[:, t % 4, b * P:(b + 1) * P], keep["w2_q"][:, t, :],
                                   start=first, stop=last)
                    if last:
                        mm.then_inc(acc_full, 1)
                if not last:
                    mm.then_inc(acc_step, 1)

            def group(g, before, now):
                for t in range(ET):
                    if now:
                        pe.wait_ge(h2_ready, g * ET + (t + 1))
                        hidden_tile(pe, g, t, u2_full, None)
                    if t < LAG:
                        if before:
                            second_layer(g * ET + t - LAG + 1, ET - LAG + t, False, t == LAG - 1)
                    elif now:
                        if t == LAG:
                            pe.wait_ge(acc_free, GB * (g + 1))
                        second_layer(g * ET + t - LAG + 1, t - LAG, t == LAG, False)

            pe.wait_ge(h_ready, GROUPS * ET + 4)
            group(0, False, True)
            with pe.Fori(1, GROUPS) as g:
                group(g, True, True)
            group(GROUPS, True, False)

        @block.scalar
        def _(act):
            act.wait_ge(scales_done, 1)
            with act.Fori(0, GROUPS) as g:
                for t in range(ET):
                    act.wait_ge(u_full, g * ET + (t + 1))
                    act.wait_ge(h_seen, g * ET + (t + 1))
                    act.activation(hidden[:, t % 2, :], u_bank(t), ACT.Gelu, bias=b1_scaled[:, t:t + 1],
                                   scale=both[:, 0:1]).then_inc(h_ready, 1)
            act.wait_ge(h_seen, GROUPS * ET + 2)
            with act.Fori(0, GROUPS) as g:
                for t in range(ET):
                    act.wait_ge(u2_full, g * ET + (t + 1))
                    act.wait_ge(h2_rounded, g * ET + (t + 1))
                    act.activation(hidden[:, t % 2, :], u_bank(t), ACT.Gelu, bias=b1_scaled[:, t:t + 1],
                                   scale=both[:, 0:1]).then_inc(h2_ready, 1)

        @block.vector
        def _(dve):
            dve.memset(start[:, 0:1], 0.0).then_inc(h_ready, 4)
            dve.memset(start[:, 1:2], 0.0).then_inc(h2_ready, 4)
            dve.memset(start[:, 2:3], 0.0).then_inc(h_seen, 2)
            dve.memset(start[:, 3:4], 0.0).then_inc(h2_rounded, 2)
            dve.memset(start[:, 4:5], 0.0).then_inc(acc_free, GB)
            dve.memset(start[:, 5:6], 0.0).then_inc(stored, 16)
            dve.tensor_copy(ident16[:], keep["ident"][:]).then_inc(ident_done, 1)

            with dve.Fori(0, GROUPS) as g:
                dve.wait_ge(loaded, g * 16 + 16)
                for b in range(LOAD):
                    op = dve.bn_stats(stats[:, b, :], x_load[:, b, :])
                op.then_inc(stats_done, 1)
                wait_apart(dve, stats_done, g + 1)
                for b in range(LOAD):
                    op = dve.bn_aggr(moments[:, b, :], stats[:, b, :])
                op.then_inc(moments_done, 1)
                dve.wait_ge(rstd_done, g + 1)
                for b in range(LOAD):
                    op = dve.tensor_scalar(normed[:, g * LOAD + b, :], x_load[:, b, :], moments[:, b, 0:1],
                                           rstd[:, b:b + 1], ALU.subtract, ALU.mult)
                op.then_inc(norm_done, 1)
                dve.wait_ge(norm_done, g + 1)
                dve.tensor_reduce(row_max[:, bass.ts(g, LOAD)], normed[:, bass.ts(g, LOAD), :], AX, ALU.max,
                                  apply_absolute_value=True).then_inc(max_done, 1)

            def activation_scale(k, maxima, weight):
                dve.tensor_reduce(peak[:, 2 * k:2 * k + 1], maxima, AX, ALU.max).then_inc(peak_own, 1)
                dve.wait_ge(peak_all, k + 1)
                dve.tensor_scalar(scale[:, k:k + 1], peak[:, 2 * k + 1:2 * k + 2], MIN_RANGE, 1.0 / QP,
                                  ALU.max, ALU.mult).then_inc(scale_step, 1)
                dve.wait_ge(scale_step, 2 * k + 1)
                dve.reciprocal(inv_scale[:, k:k + 1], scale[:, k:k + 1])
                dve.tensor_tensor(both[:, k:k + 1], scale[:, k:k + 1], keep["w_scale"][:, k:k + 1],
                                  ALU.mult).then_inc(scale_step, 1)
                dve.wait_ge(scale_step, 2 * k + 2)
                out, bias = ((b1_scaled, keep["b1_col"]), (b2_scaled, keep["b2_row"]))[k]
                dve.tensor_scalar(out[:], bias[:], both[:, k:k + 1], None, ALU.mult).then_inc(scales_done, 1)

            dve.wait_ge(max_done, GROUPS)
            activation_scale(0, row_max[:], 0)

            with dve.Fori(0, GROUPS) as g:
                dve.tensor_scalar(rounded[:], normed[:, bass.ts(g, GB), :], inv_scale[:, 0:1], MAGIC,
                                  ALU.mult, ALU.add).then_inc(xq_rounded, 1)
                dve.wait_ge(xq_rounded, g + 1)
                dve.tensor_scalar(xq[:], rounded[:], MAGIC, None, ALU.subtract).then_inc(xq_ready, 1)
                dve.wait_ge(xt_full, g + 1)
                dve.tensor_copy(xq_t[:, :, bass.ts(g, TOK)],
                                xt_bank.rearrange("p (t s) -> p t s", t=DT)).then_inc(xt_done, 1)
                for t in range(ET):
                    dve.wait_ge(h_ready, g * ET + (t + 1) + 4)
                    dve.tensor_reduce(tile_max[:, bass.ds(g * ET + t, 1)], hidden[:, t % 2, :], AX, ALU.max,
                                      apply_absolute_value=True).then_inc(h_seen, 1)

            dve.wait_ge(h_seen, GROUPS * ET + 2)
            activation_scale(1, tile_max[:], 1)

            def add_residual(n, side):
                dve.wait_ge(bias_added, n + 1)
                dve.wait_ge(stored, n * 16 + 16)
                for b in range(GB):
                    dve.wait_ge(acc_full, n * GB + (b + 1))
                    dve.scalar_tensor_tensor(result[:, b, :], psum[:, 4 + b, 0:D], both[:, 1:2],
                                             x_again[:, side, b, :], ALU.mult, ALU.add).then_inc(acc_free, 1)

            def group(g, side, before, now):
                for t in range(ET):
                    if now:
                        dve.wait_ge(h2_ready, g * ET + (t + 1) + 4)
                        dve.tensor_scalar(h_round[:, t % 2, :], hidden[:, t % 2, :], inv_scale[:, 1:2], MAGIC,
                                          ALU.mult, ALU.add).then_inc(h2_rounded, 1)
                        dve.wait_ge(h2_rounded, g * ET + (t + 1) + 2)
                        step_wait(g, t)
                        dve.tensor_scalar(h_q[:, t % 4, :], h_round[:, t % 2, :], MAGIC, None,
                                          ALU.subtract).then_inc(hq_ready, 1)
                    if before and t == LAG - 1:
                        add_residual(g - 1, side)

            def step_wait(g, t):
                if isinstance(g, int) and g == 0 and t < 4:
                    return
                if t < 4:
                    u = t + ET - 4
                    if u == ET - 1:
                        dve.wait_ge(acc_full, g * GB)
                    else:
                        dve.wait_ge(acc_step, (g - 1) * (ET - 1) + (u + 1))
                else:
                    dve.wait_ge(acc_step, g * (ET - 1) + (t - 4 + 1))

            group(0, 0, False, True)
            with dve.Fori(0, GROUPS // 2 - 1) as h:
                for side in range(2):
                    group(h * 2 + side + 1, side, True, True)
            group(GROUPS - 1, 0, True, True)
            group(GROUPS, 1, True, False)


def decoder_layer(nc, dram, out_dram):
    with ExitStack() as ctx:
        def sb(name, shape, dt=F32):
            return ctx.enter_context(nc.sbuf_tensor(name, shape, dt))

        x2_dram = nc.dram_tensor("x2_residual", (NB, P, D), F32, kind="Internal").ap()
        psum = ctx.enter_context(nc.psum_tensor("banks", [P, 8, 512], F32))
        keep = {
            "ident": sb("ident", [P, P]),
            "w1_q": sb("w1_q", [P, DT, INNER], BF16),
            "w2_q": sb("w2_q", [P, ET, D], BF16),
            "w_scale": sb("w_scale", [P, 2]),
            "b1_col": sb("b1_col", [P, ET]),
            "b2_row": sb("b2_row", [P, D]),
            "half4": sb("half4", [P, 4]),
        }
        keep["half"] = keep["half4"][:, 0:2]
        with ExitStack() as inner:
            def weight(name, shape, dt=F32):
                keep[name] = inner.enter_context(nc.sbuf_tensor(name, shape, dt))

            weight("causal", [P, P])
            weight("bo_row", [P, D])
            weight("g_bias", [P, DT])
            weight("qk_bias", [P, 1])
            weight("third", [P, 2, 3])
            weight("negs", [P, 2, 3])
            weight("fold_qk", [P, 2, DT, D], F32R)
            weight("fold_vo", [P, 2, DT, FW], F32R)
            for n in ("Wq", "Wk", "Wv"):
                weight("cross_" + n, [P, 2, DT, INNER], F32R)
            weight("cross_Wo", [P, 2, ET, D], F32R)
            prepare_weights(nc, dram, keep, psum)
            attentions(nc, dram, keep, psum, x2_dram)
        feed_forward(nc, keep, psum, x2_dram, out_dram)


NAMES = {"x": "x", "ctx_1024": "ctx", "fside_Bx1xSxS2_0": "mask"}
INS = ["x", "ctx_1024", "fside_Bx1xSxS2_0", "L0_attn_Wq", "L0_attn_bq", "L0_attn_Wk", "L0_attn_bk", "L0_attn_Wv",
       "L0_attn_bv", "L0_attn_Wo", "L0_attn_bo", "L0_xattn_Wq", "L0_xattn_Wk", "L0_xattn_Wv", "L0_xattn_Wo",
       "L0_ffn_w1", "L0_ffn_b1", "L0_ffn_w2", "L0_ffn_b2"]


def kernel(**inputs):
    import numpy as np
    import concourse.bacc as bacc
    from concourse.bass_utils import run_bass_kernel_spmd

    nc = bacc.Bacc("TRN2", target_bir_lowering=False, num_devices=1)
    arrays, dram = {}, {}
    for name in INS:
        a = np.ascontiguousarray(inputs[name])
        arrays[f"in_{name}_dram"] = a
        short = NAMES.get(name, name.removeprefix("L0_"))
        dram[short] = nc.dram_tensor(f"in_{name}_dram", a.shape, mybir.dt.from_np(a.dtype), kind="ExternalInput").ap()
    out = nc.dram_tensor("out_0_dram", (NB, P, D), F32, kind="ExternalOutput").ap()
    decoder_layer(nc, dram, out)
    r = run_bass_kernel_spmd(nc, [arrays], core_ids=[0])
    return r.results[0]["out_0_dram"]
```

```python
from contextlib import ExitStack

import concourse.bass as bass
from concourse import mybir

F32 = mybir.dt.float32
F32R = mybir.dt.float32r
F16 = mybir.dt.float16
BF16 = mybir.dt.bfloat16
ALU = mybir.AluOpType
ACT = mybir.ActivationFunctionType
AX = mybir.AxisListType.X
RMAX = bass.bass_isa.ReduceOp.max

P = 128
D = 256
DT = D // P
NB = 64
PAIRS = NB // 2
HEADS = 16
DH = 64
INNER = HEADS * DH
ET = INNER // P
GROUP = 4
TOP_K = 64
QUAD = 4
QUADS = 2 * HEADS // QUAD
VW = DH + 2
FW = D + 2
NEG = -3.0e38
MASKED = -1.0e30
EPS = 1e-5
QP = 127.0
MIN_RANGE = 1e-6
MAGIC = 12582912.0
HI, LO = 0, 1
FREE = 2

(J_Q1, J_K0, J_Q2, J_Q3, J_K1, J_K2, J_K3, J_VV0, J_X, J_G, J_PT0, J_VV1, J_PT1, J_AO, J_V0, J_V1, J_VV2,
 J_RAW, J_X1, J_VV3, J_Q0, J_CTX) = range(22)
FJ = 22
J_Q, J_K = (J_Q0, J_Q1, J_Q2, J_Q3), (J_K0, J_K1, J_K2, J_K3)
J_VV = (J_VV0, J_VV1, J_VV2, J_VV3)
KV = (J_K0, J_K1, J_K2, J_K3, J_VV0, J_VV1, J_VV2, J_VV3)
OF_LAST_PAIR = (J_Q1, J_Q2, J_Q3)
OF_NEXT_PAIR = (J_X, J_G, J_V0, J_V1, J_RAW, J_CTX)
same_bank = lambda k: range(k % 2, FJ, 2)
WITH_HI = [k for k in range(FJ) if k not in (J_RAW, J_AO, *KV)]
BACK = ["pv0", "pv1", "pv2", "ct0", "pv3", "ct1", "pv4", "pv5", "out0", "pv6", "ct2", "pv7", "ct3", "out1"]
BJ = len(BACK)


def runs(k, front, back, ahead):
    return back if k in OF_LAST_PAIR else ahead if k in OF_NEXT_PAIR else front


def left_out(k, jobs, *halves):
    before = jobs[:jobs.index(k)]
    return next((n for n, m in enumerate(reversed(before)) if runs(m, *halves)), len(before))


def steps(k, jobs, *halves):
    after = jobs[jobs.index(k) + 1:]
    return 1 + left_out(k, jobs, *halves) + (0 if any(runs(m, *halves) for m in after) else len(after))


def wait_apart(eng, sem, value):
    value = value if isinstance(value, int) else eng.to_reg(value)
    eng.wait_ge(sem, 1)
    eng.wait_ge(sem, value)


def split_products(pe, out, lhs, rhs, last=True, first=True):
    pe.matmul(out, lhs[HI], rhs[HI], start=first, stop=False)
    pe.matmul(out, lhs[HI], rhs[LO], start=False, stop=False)
    return pe.matmul(out, lhs[LO], rhs[HI], start=False, stop=last)


def prepare_weights(nc, dram, keep, psum):
    with ExitStack() as ctx:
        def sb(name, shape, dt=F32):
            return ctx.enter_context(nc.sbuf_tensor(name, shape, dt))

        def sem(name):
            return ctx.enter_context(nc.semaphore(name))

        attn_w = {n: sb(f"w_{n}", [P, DT, D]) for n in ("Wq", "Wk", "Wv", "Wo")}
        attn_t = {n: sb(f"wt_{n}", [P, DT, D]) for n in ("Wq", "Wk", "Wv")}
        cross = {n: sb(f"cw_{n}", [P, ET, D]) for n in ("Wq", "Wk", "Wv")}
        cross_o = sb("cw_Wo", [P, DT, INNER])
        w1 = sb("w1_nat", [P, ET, D])
        w2 = sb("w2_nat", [P, DT, INNER])
        bias = {n: sb(f"b_{n}", [P, DT]) for n in ("bq", "bk", "bv")}
        bias_rows = {n: sb(f"br_{n}", [P, DT, P]) for n in ("bq", "bv")}
        wabs = sb("wabs", [P, 2])
        wmax = sb("wmax", [P, 2])
        winv = sb("winv", [P, 2])

        attn_loaded = sem("attn_loaded")
        bias_loaded = sem("bias_loaded")
        cross_loaded = sem("cross_loaded")
        ffn_loaded = sem("ffn_loaded")
        ident_zero, ident_ready = sem("ident_zero"), sem("ident_ready")
        causal_zero, causal_ready = sem("causal_zero"), sem("causal_ready")
        rows_ready = sem("rows_ready")
        job_full, job_hi, job_done = sem("job_full"), sem("job_hi"), sem("job_done")
        abs_ready, abs_all = sem("abs_ready"), sem("abs_all")
        scale_step = sem("scale_step")
        quant_step, quantised = sem("quant_step"), sem("quantised")
        u_hi = sem("u_hi")
        bank_of = lambda n: psum[:, n % 4, :]

        N_T, N_A, N_VO, N_COL, N_ROW, N_CROSS, N_FFN, N_JOBS = 0, 3, 4, 5, 6, 7, 23, 31
        TWICE = [N_A, N_VO] + list(range(N_CROSS, N_FFN))
        hi_count = lambda n: TWICE.index(n) + 1
        cross_jobs = [(n, kt, g) for n in ("Wq", "Wk", "Wv") for kt in range(DT) for g in range(2)]

        block = ctx.enter_context(nc.Block())

        @block.sync
        def _(sp):
            for n in ("Wq", "Wk", "Wv", "Wo"):
                sp.dma_start(attn_w[n][:], dram["attn_" + n].rearrange("(t p) e -> p t e", p=P)).then_inc(attn_loaded, 16)
            for n in ("Wq", "Wk", "Wv"):
                sp.dma_start(cross[n][:], dram["xattn_" + n].rearrange("(t p) d -> p t d", p=P)).then_inc(cross_loaded, 16)
            sp.dma_start(cross_o[:], dram["xattn_Wo"].rearrange("(t p) e -> p t e", p=P)).then_inc(cross_loaded, 16)
            sp.wait_ge(bias_loaded, 16 * 6)

        @block.gpsimd
        def _(pool):
            pool.memset(keep["ident"][:], 0.0).then_inc(ident_zero, 1)
            pool.memset(keep["causal"][:], 0.0).then_inc(causal_zero, 1)
            pool.wait_ge(ident_zero, 1)
            pool.affine_select(out=keep["ident"][:], in_=keep["ident"][:], compare_op=ALU.not_equal, fill=1.0,
                               base=0, pattern=[[-1, P]], channel_multiplier=1).then_inc(ident_ready, 1)
            pool.wait_ge(causal_zero, 1)
            pool.affine_select(out=keep["causal"][:], in_=keep["causal"][:], compare_op=ALU.is_ge, fill=MASKED,
                               base=0, pattern=[[-1, P]], channel_multiplier=1).then_inc(causal_ready, 1)
            pool.memset(keep["half4"][:], -0.5)
            for k in range(2):
                pool.wait_ge(abs_ready, k + 1)
                pool.partition_all_reduce(wmax[:, k:k + 1], wabs[:, k:k + 1], P, RMAX).then_inc(abs_all, 1)
            pool.wait_ge(causal_ready, 1)

        @block.scalar
        def _(act):
            with nc.allow_non_contiguous_dma(reason="bias columns"):
                for n in ("bq", "bk", "bv"):
                    act.dma_start(bias[n][:], dram["attn_" + n].rearrange("(t p) -> p t", p=P)).then_inc(bias_loaded, 16)
                act.dma_start(keep["bo_row"][:], dram["attn_bo"].rearrange("(a d) -> a d", a=1).to_broadcast([P, D])).then_inc(bias_loaded, 16)
                act.dma_start(keep["b1_col"][:], dram["ffn_b1"].rearrange("(t p) -> p t", p=P)).then_inc(bias_loaded, 16)
                act.dma_start(keep["b2_row"][:], dram["ffn_b2"].rearrange("(a d) -> a d", a=1).to_broadcast([P, D])).then_inc(bias_loaded, 16)
            act.dma_start(w1[:], dram["ffn_w1"].rearrange("(t p) d -> p t d", p=P)).then_inc(ffn_loaded, 16)
            act.dma_start(w2[:], dram["ffn_w2"].rearrange("(t p) h -> p t h", p=P)).then_inc(ffn_loaded, 16)

            def hi_part(n, dst, src):
                act.wait_ge(job_full, n + 1)
                act.activation(dst, src, ACT.Copy).then_inc(job_hi, 1)

            hi_part(N_A, keep["fold_qk"][:, HI], bank_of(N_A).rearrange("p (t d) -> p t d", t=DT))
            hi_part(N_VO, keep["fold_vo"][:, HI, :, 0:D], bank_of(N_VO).rearrange("p (t d) -> p t d", t=DT))
            for k, (n, kt, g) in enumerate(cross_jobs):
                hi_part(N_CROSS + k, keep["cross_" + n][:, HI, kt, 512 * g:512 * (g + 1)], bank_of(N_CROSS + k))
            for g in range(4):
                n = N_CROSS + 12 + g
                hi_part(n, keep["cross_Wo"][:, HI, 2 * g:2 * g + 2, :], bank_of(n).rearrange("p (t d) -> p t d", t=2))

        @block.tensor
        def _(pe):
            ident = keep["ident"]

            def begin(n):
                if n >= 4:
                    pe.wait_ge(job_done, n - 3)
                return bank_of(n)

            pe.wait_ge(ident_ready, 1)
            pe.wait_ge(attn_loaded, 64)
            for k, n in enumerate(("Wq", "Wk", "Wv")):
                bank = begin(N_T + k)
                for et in range(DT):
                    for dt in range(DT):
                        mm = pe.transpose(bank[:, et * D + dt * P:et * D + (dt + 1) * P],
                                          attn_w[n][:, dt, et * P:(et + 1) * P], ident[:])
                mm.then_inc(job_full, 1)
            for n, left, right in ((N_A, attn_t["Wq"], attn_t["Wk"]), (N_VO, attn_t["Wv"], attn_w["Wo"])):
                bank = begin(n)
                pe.wait_ge(job_done, 3)
                for dt in range(DT):
                    for et in range(DT):
                        mm = pe.matmul(bank[:, dt * D:(dt + 1) * D], left[:, et, dt * P:(dt + 1) * P], right[:, et, :],
                                       start=(et == 0), stop=(et == DT - 1))
                mm.then_inc(job_full, 1)
            bank = begin(N_COL)
            pe.wait_ge(bias_loaded, 16 * 6)
            pe.wait_ge(rows_ready, 2)
            for dt in range(DT):
                for et in range(DT):
                    pe.matmul(bank[:, dt:dt + 1], attn_t["Wq"][:, et, dt * P:(dt + 1) * P], bias["bk"][:, et:et + 1],
                              start=(et == 0), stop=(et == DT - 1))
            for dt in range(DT):
                for et in range(DT):
                    pe.matmul(bank[:, 2 + dt:3 + dt], attn_t["Wk"][:, et, dt * P:(dt + 1) * P], bias["bq"][:, et:et + 1],
                              start=(et == 0), stop=(et == DT - 1))
            for et in range(DT):
                mm = pe.matmul(bank[:, 4:5], bias_rows["bq"][:, et, :], bias["bk"][:, et:et + 1],
                               start=(et == 0), stop=(et == DT - 1))
            mm.then_inc(job_full, 1)
            bank = begin(N_ROW)
            for et in range(DT):
                mm = pe.matmul(bank[:, 0:D], bias_rows["bv"][:, et, :], attn_w["Wo"][:, et, :],
                               start=(et == 0), stop=(et == DT - 1))
            mm.then_inc(job_full, 1)
            pe.wait_ge(cross_loaded, 64)
            for k, (n, kt, g) in enumerate(cross_jobs):
                bank = begin(N_CROSS + k)
                for r in range(4):
                    mm = pe.transpose(bank[:, r * P:(r + 1) * P], cross[n][:, 4 * g + r, kt * P:(kt + 1) * P], ident[:])
                mm.then_inc(job_full, 1)

            def transpose_wide(n, src, g):
                bank = begin(n)
                for t in range(2):
                    for dt in range(DT):
                        et = 2 * g + t
                        mm = pe.transpose(bank[:, t * D + dt * P:t * D + (dt + 1) * P],
                                          src[:, dt, et * P:(et + 1) * P], ident[:])
                mm.then_inc(job_full, 1)

            for g in range(4):
                transpose_wide(N_CROSS + 12 + g, cross_o, g)
            pe.wait_ge(quantised, 1)
            for kt in range(DT):
                for g in range(2):
                    bank = begin(N_FFN + 2 * kt + g)
                    for r in range(4):
                        mm = pe.transpose(bank[:, r * P:(r + 1) * P], w1[:, 4 * g + r, kt * P:(kt + 1) * P], ident[:])
                    mm.then_inc(job_full, 1)
            pe.wait_ge(quantised, 2)
            for g in range(4):
                transpose_wide(N_FFN + 4 + g, w2, g)

        @block.vector
        def _(dve):
            dve.wait_ge(bias_loaded, 16 * 6)
            for n in ("bq", "bv"):
                dve.tensor_copy(bias_rows[n][:], bias[n][:].unsqueeze(2).to_broadcast([P, DT, P])).then_inc(rows_ready, 1)
            dve.memset(keep["fold_vo"][:, :, :, D + 1:FW].bitcast(F32), 0.0)
            dve.memset(keep["third"][:, :, 0:2], 1.0 / 3.0)
            dve.memset(keep["third"][:, :, 2:3], 1.0 / (3.0 * GROUP))
            dve.memset(keep["negs"][:, :, 0:2], -1.0)
            dve.memset(keep["negs"][:, :, 2:3], -1.0 / GROUP)

            def full(n):
                dve.wait_ge(job_full, n + 1)
                return bank_of(n)

            for k, n in enumerate(("Wq", "Wk", "Wv")):
                dve.tensor_copy(attn_t[n][:].rearrange("p t d -> p (t d)"), full(N_T + k)).then_inc(job_done, 1)

            dve.wait_ge(ffn_loaded, 32)
            for k, w in enumerate((w1, w2)):
                dve.tensor_reduce(wabs[:, k:k + 1], w[:].rearrange("p t d -> p (t d)"), AX, ALU.max,
                                  apply_absolute_value=True).then_inc(abs_ready, 1)

            def lo_part(n, dst, src, hi):
                dve.wait_ge(job_hi, hi_count(n))
                dve.tensor_tensor(dst, src, hi.bitcast(F32), ALU.subtract).then_inc(job_done, 1)

            for n, w, m in ((N_A, keep["fold_qk"], D), (N_VO, keep["fold_vo"], D)):
                src = full(n).rearrange("p (t d) -> p t d", t=DT)
                lo_part(n, w[:, LO, :, 0:m], src, w[:, HI, :, 0:m])
            bank = full(N_COL)
            u = bank[:, 0:2].unsqueeze(2)
            dve.tensor_copy(keep["fold_vo"][:, HI, :, D:D + 1], u).then_inc(u_hi, 1)
            dve.tensor_copy(keep["g_bias"][:], bank[:, 2:4])
            dve.tensor_copy(keep["qk_bias"][:], bank[:, 4:5])
            dve.wait_ge(u_hi, 1)
            dve.tensor_tensor(keep["fold_vo"][:, LO, :, D:D + 1], u, keep["fold_vo"][:, HI, :, D:D + 1].bitcast(F32),
                              ALU.subtract).then_inc(job_done, 1)
            bank = full(N_ROW)
            dve.tensor_tensor(keep["bo_row"][:], bank[:, 0:D], keep["bo_row"][:], ALU.add).then_inc(job_done, 1)

            def quantise(k, w):
                dve.wait_ge(abs_all, k + 1)
                dve.tensor_scalar(keep["w_scale"][:, k:k + 1], wmax[:, k:k + 1], MIN_RANGE, 1.0 / QP,
                                  ALU.max, ALU.mult).then_inc(scale_step, 1)
                dve.wait_ge(scale_step, 2 * k + 1)
                dve.reciprocal(winv[:, k:k + 1], keep["w_scale"][:, k:k + 1]).then_inc(scale_step, 1)
                dve.wait_ge(scale_step, 2 * k + 2)
                dve.tensor_scalar(w[:], w[:], winv[:, k:k + 1], MAGIC, ALU.mult, ALU.add).then_inc(quant_step, 1)
                dve.wait_ge(quant_step, k + 1)
                dve.tensor_scalar(w[:], w[:], MAGIC, None, ALU.subtract).then_inc(quantised, 1)

            for k, (n, kt, g) in enumerate(cross_jobs):
                w = keep["cross_" + n]
                lo_part(N_CROSS + k, w[:, LO, kt, 512 * g:512 * (g + 1)], full(N_CROSS + k),
                        w[:, HI, kt, 512 * g:512 * (g + 1)])
                if k == 3:
                    quantise(0, w1)
                if k == 7:
                    quantise(1, w2)
            for g in range(4):
                n = N_CROSS + 12 + g
                w = keep["cross_Wo"]
                lo_part(n, w[:, LO, 2 * g:2 * g + 2, :], full(n).rearrange("p (t d) -> p t d", t=2),
                        w[:, HI, 2 * g:2 * g + 2, :])
            for kt in range(DT):
                for g in range(2):
                    dve.tensor_copy(keep["w1_q"][:, kt, 512 * g:512 * (g + 1)],
                                    full(N_FFN + 2 * kt + g)).then_inc(job_done, 1)
            for g in range(4):
                dve.tensor_copy(keep["w2_q"][:, 2 * g:2 * g + 2, :].rearrange("p t d -> p (t d)"),
                                full(N_FFN + 4 + g)).then_inc(job_done, 1)


def attentions(nc, dram, keep, psum, x2_dram):
    with ExitStack() as ctx:
        def sb(name, shape, dt=F32):
            return ctx.enter_context(nc.sbuf_tensor(name, shape, dt))

        def sem(name):
            return ctx.enter_context(nc.semaphore(name))

        x_in = sb("x_in", [P, 2, D])
        ctx_in = sb("ctx_in", [P, 2, D])
        x_bias = sb("x_bias", [P, 2, D])
        xn = sb("xn", [P, 2, D])
        ctx_t = sb("ctx_t", [P, 2, DT, 2 * P], F32R)
        xn_t = sb("xn_t", [P, 2, DT, 2 * P], F32R)
        g_t = sb("g_t", [P, 2, DT, 2 * P], F32R)
        v_fold = sb("v_fold", [P, 2, 2, D], F32R)
        raw = sb("raw", [P, 2, P])
        left = sb("left", [P, 2, P])
        top8 = sb("top8", [P, 2, 8])
        win_in = sb("win_in", [P, 2, P])
        sparse_in = sb("sparse_in", [P, 2, P])
        comp_in = sb("comp_in", [P, 2, P // GROUP])
        win_e = sb("win_e", [P, 2, P])
        sparse_e = sb("sparse_e", [P, 2, P])
        comp_e = sb("comp_e", [P, 2, P // GROUP])
        maxes = sb("maxes", [P, 2, 3])
        neg_maxes = sb("neg_maxes", [P, 2, 3])
        sums = sb("sums", [P, 2, 3])
        inv_sums = sb("inv_sums", [P, 2, 3])
        weights = sb("weights", [P, 2, 3])
        probs = sb("probs", [P, 2, P])
        probs_t = sb("probs_t", [P, 2, 2, P], F32R)
        x1 = sb("x1", [P, 2, D])
        x1_old = sb("x1_old", [P, 2, D])
        xn1 = sb("xn1", [P, 2, D])
        xn1_t = sb("xn1_t", [P, 2, DT, 2 * P], F32R)
        row_rq = sb("row_rq", [P, 2])
        stats = sb("stats", [P, 2, 6])
        moments = sb("moments", [P, 2, 2])
        var_eps = sb("var_eps", [P, 2])
        rstd = sb("rstd", [P, 2])
        stats1 = sb("stats1", [P, 2, 6])
        moments1 = sb("moments1", [P, 2, 2])
        var_eps1 = sb("var_eps1", [P, 2])
        rstd1 = sb("rstd1", [P, 2])
        start = sb("start", [P, 13])
        q_t = sb("q_t", [P, 2, 4, 2 * P], F16)
        k_t = sb("k_t", [P, 2, ET, 2 * P], F16)
        q_stack = sb("q_stack", [P, 2, ET, 2 * P], F16)
        k_stack = sb("k_stack", [P, 2, 2, ET, 2 * P], F16)
        kv_copy = sb("kv_copy", [P, 2, 512])
        v_nat = sb("v_nat", [P, 2, 2, HEADS, VW], F16)
        mask = sb("mask", [P, 2, P])
        scores = sb("scores", [P, 2, QUAD, P])
        score_max = sb("score_max", [P, 2, QUAD])
        neg_max = sb("neg_max", [P, 2, QUAD])
        expd = sb("expd", [P, 2, QUAD, P])
        exp_copy = sb("exp_copy", [P, 2, QUAD, P])
        exp_t = sb("exp_t", [P, 2, 2, QUAD, P], F16)
        inv_den = sb("inv_den", [P, 2, QUAD])
        heads_out = sb("heads_out", [P, 2, 2 * QUAD * DH])
        heads_t = sb("heads_t", [P, 2, ET, P], F32R)
        x2 = sb("x2", [P, 2, D])

        fj_bank = lambda k: psum[:, k % 2, :]
        sc_bank = lambda q: psum[:, 2 + q % 2, :]
        et_bank = lambda q: psum[:, 4 + q % 2, :]
        bj_bank = lambda k: psum[:, 6 + k % 2, :]

        x_loaded, ctx_loaded = sem("x_loaded"), sem("ctx_loaded")
        mask_loaded = [sem("mask_loaded0"), sem("mask_loaded1")]
        q_stacked = [sem(f"q_stacked{n}") for n in range(4)]
        k_stacked = sem("k_stacked")
        x2_free = [sem("x2_free0"), sem("x2_free1")]
        fj_full, fj_hi, fj_free = sem("fj_full"), sem("fj_hi"), [sem("fj_free0"), sem("fj_free1")]
        sc_full, sc_free = sem("sc_full"), sem("sc_free")
        et_full, et_free = sem("et_full"), sem("et_free")
        exp_split, kv_split = sem("exp_split"), sem("kv_split")
        bj_full, bj_hi, bj_free = sem("bj_full"), sem("bj_hi"), sem("bj_free")
        stats_x, moments_x, eps_x, rstd_x, xn_ready = (sem(n) for n in ("stats_x", "moments_x", "eps_x", "rstd_x", "xn_ready"))
        stats_x1, moments_x1, eps_x1, rstd_x1, xn1_ready = (sem(n) for n in ("stats_x1", "moments_x1", "eps_x1", "rstd_x1", "xn1_ready"))
        x_bias_ready, x1_kept = sem("x_bias_ready"), sem("x1_kept")
        rq_ready, top_found, top_out = sem("rq_ready"), sem("top_found"), sem("top_out")
        comp_ready, sparse_ready, max_ready, softmax_in = sem("comp_ready"), sem("sparse_ready"), sem("max_ready"), sem("softmax_in")
        softmax_exp, inv_ready, weights_ready, mix_a_ready, mix_b_ready, probs_ready = (
            sem(n) for n in ("softmax_exp", "inv_ready", "weights_ready", "mix_a_ready", "mix_b_ready", "probs_ready"))
        scores_ready, exp_ready, den_ready = sem("scores_ready"), sem("exp_ready"), sem("den_ready")

        fj = lambda i, k: (i + 1) * FJ + (k + 1)
        fj_his = lambda i, k: (i + 1) * len(WITH_HI) + (WITH_HI.index(k) + 1)
        bj = lambda j, name: j * BJ + (BACK.index(name) + 1)
        bj_his = lambda j, c: j * 4 + (c + 1)
        quad = lambda j, q: j * QUADS + (q + 1)
        kv = lambda i, k: i * len(KV) + (KV.index(k) + 1)
        fj_left = lambda i, k: (i + 1) * (FJ // 2) + (k // 2 + 2)
        hilo = lambda t, *at: (t[(slice(None), HI, *at)], t[(slice(None), LO, *at)])
        tok = lambda b: slice(b * P, (b + 1) * P)
        tile = lambda t: slice(t * P, (t + 1) * P)

        def landing(k):
            bank = fj_bank(k)
            pair = bank.rearrange("p (t s) -> p t s", t=2)
            if k == J_CTX:
                return ctx_t, (), pair
            if k == J_X:
                return xn_t, (), pair
            if k == J_X1:
                return xn1_t, (), pair
            if k in (J_V0, J_V1):
                return v_fold, (int(k == J_V1),), bank[:, 0:D]
            if k in J_K or k in J_Q:
                n = J_K.index(k) if k in J_K else J_Q.index(k) % 2
                return (k_t if k in J_K else q_t), (slice(2 * n, 2 * n + 2),), pair
            if k in (J_PT0, J_PT1):
                return probs_t, (int(k == J_PT1),), bank[:, 0:P]
            n = J_VV.index(k)
            half = HEADS // 2
            return (v_nat, (n // 2, slice(half * (n % 2), half * (n % 2) + half), slice(0, DH)),
                    bank.rearrange("p (h d) -> p h d", d=DH))

        block = ctx.enter_context(nc.Block())

        @block.sync
        def _(sp):
            x_pairs = dram["x"].rearrange("(i b) s d -> i s b d", b=2)
            ctx_pairs = dram["ctx"].rearrange("(i b) s d -> i s b d", b=2)
            mask_rows = dram["mask"].rearrange("(i b) one s k -> i b (one s) k", b=2)
            x2_rows = x2_dram.rearrange("(i b) s d -> i b s d", b=2)

            def stack_queries(i, n):
                wait_apart(sp, fj_free[J_Q[n] % 2], fj_left(i, J_Q[n]))
                for part in (HI, LO):
                    for parity in range(2):
                        sp.dma_start(q_stack[64 * part:64 * part + 64, parity, 2 * n:2 * n + 2],
                                     q_t[64 * parity:64 * parity + 64, part, 2 * (n % 2):2 * (n % 2) + 2]).then_inc(q_stacked[n], 16)

            def body(i, front, back, ahead):
                j = i - 1
                if back:
                    for n in range(1, 4):
                        stack_queries(i, n)
                if ahead:
                    wait_apart(sp, xn_ready, i + 1)
                    wait_apart(sp, x_bias_ready, i + 1)
                    sp.dma_start(x_in[:], x_pairs[i + 1]).then_inc(x_loaded, 16)
                    wait_apart(sp, fj_full, fj(i - 1, J_CTX))
                    sp.dma_start(ctx_in[:], ctx_pairs[i + 1]).then_inc(ctx_loaded, 16)
                if back:
                    if front:
                        wait_apart(sp, sc_free, quad(j, 3) + FREE)
                        sp.dma_start(mask[:, 0, :], mask_rows[i, 0]).then_inc(mask_loaded[0], 16)
                if front:
                    wait_apart(sp, kv_split, kv(i, J_K3) + FREE)
                    if back:
                        wait_apart(sp, sc_full, quad(j, 7))
                    for part in (HI, LO):
                        for parity in range(2):
                            for half in range(2):
                                sp.dma_start(k_stack[64 * half:64 * half + 64, part, parity],
                                             k_t[64 * parity:64 * parity + 64, part]).then_inc(k_stacked, 16)
                if back:
                    wait_apart(sp, bj_free, bj(j, "out0") + FREE)
                    sp.dma_start(x2_rows[j, 0], x2[:, 0, :]).then_inc(x2_free[0], 16)
                    if front:
                        wait_apart(sp, sc_free, quad(j, 7) + FREE)
                        sp.dma_start(mask[:, 1, :], mask_rows[i, 1]).then_inc(mask_loaded[1], 16)
                if front:
                    stack_queries(i, 0)
                if back:
                    wait_apart(sp, bj_free, bj(j, "out1") + FREE)
                    sp.dma_start(x2_rows[j, 1], x2[:, 1, :]).then_inc(x2_free[1], 16)

            sp.dma_start(x_in[:], x_pairs[0]).then_inc(x_loaded, 16)
            sp.dma_start(ctx_in[:], ctx_pairs[0]).then_inc(ctx_loaded, 16)
            for b in range(2):
                sp.dma_start(mask[:, b, :], mask_rows[0, b]).then_inc(mask_loaded[b], 16)
            body(0, True, False, True)
            with sp.Fori(1, PAIRS - 1) as i:
                body(i, True, True, True)
            body(PAIRS - 1, True, True, False)
            body(PAIRS, False, True, False)
            for b in range(2):
                wait_apart(sp, x2_free[b], 16 * (PAIRS + 1))

        @block.gpsimd
        def _(pool):
            def reciprocal_deviation(i, moments_done, mom, ve, eps_done, out, done):
                wait_apart(pool, moments_done, i + 1)
                pool.tensor_scalar(ve[:], mom[:, :, 1], EPS, None, ALU.add).then_inc(eps_done, 1)
                pool.wait_ge(eps_done, i + 1)
                pool.tensor_tensor(out[:], ve[:], keep["half"], ALU.pow).then_inc(done, 1)

            def body(i, front, back, ahead):
                j = i - 1

                def lo(k):
                    dst, at, _ = landing(k)
                    src = kv_copy[:, KV.index(k) % 2, :]
                    src = src.rearrange("p (t s) -> p t s", t=2) if k in J_K else src.rearrange("p (h d) -> p h d", d=DH)
                    pool.wait_ge(fj_free[k % 2], fj_left(i, k))
                    pool.tensor_tensor(hilo(dst, *at)[LO], src, hilo(dst, *at)[HI], ALU.subtract).then_inc(kv_split, 1)

                def exp_lo(q):
                    pool.wait_ge(et_free, quad(j, q) + FREE)
                    pool.tensor_tensor(exp_t[:, q % 2, LO], exp_copy[:, q % 2], exp_t[:, q % 2, HI],
                                       ALU.subtract).then_inc(exp_split, 1)

                if back:
                    wait_apart(pool, bj_free, bj(i - 2, "out1") + FREE)
                    wait_apart(pool, fj_free[J_AO % 2], fj_left(i - 1, J_AO))
                    pool.tensor_copy(x1_old[:], x1[:]).then_inc(x1_kept, 1)
                if front:
                    if not back:
                        pool.wait_ge(x_loaded, 16 * (i + 1))
                    for b in range(2):
                        op = pool.tensor_tensor(x_bias[:, b, :], x_in[:, b, :], keep["bo_row"][:], ALU.add)
                    op.then_inc(x_bias_ready, 1)
                if front:
                    lo(J_K0)
                    lo(J_K1)
                if back:
                    exp_lo(0)
                if front:
                    lo(J_K2)
                if back:
                    exp_lo(1)
                if ahead:
                    reciprocal_deviation(i + 1, moments_x, moments, var_eps, eps_x, rstd, rstd_x)
                if front:
                    lo(J_K3)
                if back:
                    exp_lo(2)
                    exp_lo(3)
                if front:
                    lo(J_VV0)
                if back:
                    exp_lo(4)
                    exp_lo(5)
                if front:
                    lo(J_VV1)
                if back:
                    exp_lo(6)
                    exp_lo(7)
                if front:
                    reciprocal_deviation(i, moments_x1, moments1, var_eps1, eps_x1, rstd1, rstd_x1)
                    lo(J_VV2)
                    lo(J_VV3)

            body(-1, False, False, True)
            body(0, True, False, True)
            with pool.Fori(1, PAIRS - 1) as i:
                body(i, True, True, True)
            body(PAIRS - 1, True, True, False)
            body(PAIRS, False, True, False)

        @block.tensor
        def _(pe):
            ident = keep["ident"][:]

            def body(i, front, back, ahead):
                j = i - 1

                def begin(k):
                    pe.wait_ge(fj_free[k % 2], fj_left(i, k) - (1 + left_out(k, same_bank(k), front, back, ahead)))
                    return fj_bank(k)

                def done(mm, k):
                    mm.then_inc(fj_full, steps(k, range(FJ), front, back, ahead))

                def evacuated(k):
                    pe.wait_ge(fj_free[k % 2], fj_left(i, k))

                def transpose_pair(k, src):
                    bank = begin(k)
                    for dt in range(DT):
                        for b in range(2):
                            mm = pe.transpose(bank[:, tile(2 * dt + b)], src[:, b, tile(dt)], ident)
                    done(mm, k)

                def project(k, out_tiles, w, src):
                    bank = begin(k)
                    for m, mt in enumerate(out_tiles):
                        for kt in range(DT):
                            mm = split_products(pe, bank[:, m * 2 * P:(m + 1) * 2 * P], hilo(w, kt, tile(mt)),
                                                hilo(src, kt), first=(kt == 0), last=(kt == DT - 1))
                    done(mm, k)

                def context_transpose():
                    pe.wait_ge(ctx_loaded, 16 * (i + 2))
                    transpose_pair(J_CTX, ctx_in)

                def x_transpose():
                    pe.wait_ge(xn_ready, i + 2)
                    transpose_pair(J_X, xn)

                def fold_query():
                    evacuated(J_X)
                    project(J_G, range(DT), keep["fold_qk"], xn_t)

                def fold_value(b):
                    bank = begin(J_V0 if b == 0 else J_V1)
                    for kt in range(DT):
                        mm = split_products(pe, bank[:, 0:FW], hilo(xn_t, kt, tok(b)), hilo(keep["fold_vo"], kt),
                                            first=(kt == 0), last=(kt == DT - 1))
                    done(mm, J_V0 if b == 0 else J_V1)

                def raw_scores():
                    evacuated(J_G)
                    bank = begin(J_RAW)
                    for b in range(2):
                        for kt in range(DT):
                            mm = split_products(pe, bank[:, b * 2 * P:(b + 1) * 2 * P], hilo(g_t, kt, tok(b)),
                                                hilo(xn_t, kt), first=(kt == 0), last=(kt == DT - 1))
                    done(mm, J_RAW)

                def keys(n):
                    pe.wait_ge(fj_free[J_CTX % 2], fj_left(i - 1, J_CTX))
                    project(J_K[n], (2 * n, 2 * n + 1), keep["cross_Wk"], ctx_t)

                def values(n):
                    k, b, half = J_VV[n], n // 2, n % 2
                    bank = begin(k)
                    for kt in range(DT):
                        mm = split_products(pe, bank, hilo(ctx_t, kt, tok(b)),
                                            hilo(keep["cross_Wv"], kt, slice(half * 512, half * 512 + 512)),
                                            first=(kt == 0), last=(kt == DT - 1))
                    done(mm, k)

                def probs_transpose(b):
                    pe.wait_ge(probs_ready, i * 2 + (b + 1))
                    k = (J_PT0, J_PT1)[b]
                    bank = begin(k)
                    done(pe.transpose(bank[:, 0:P], probs[:, b, :], ident), k)

                def attend():
                    evacuated(J_PT1)
                    bank = begin(J_AO)
                    for b in range(2):
                        mm = split_products(pe, bank[:, b * D:(b + 1) * D], hilo(probs_t, b), hilo(v_fold, b))
                    done(mm, J_AO)

                def x1_transpose():
                    pe.wait_ge(xn1_ready, i + 1)
                    transpose_pair(J_X1, xn1)

                def queries(n):
                    if n == 0:
                        evacuated(J_X1)
                    project(J_Q[n], (2 * n, 2 * n + 1), keep["cross_Wq"], xn1_t)

                def score(q):
                    if q == 0:
                        pe.wait_ge(k_stacked, j * 128 + 128)
                    if q < 4:
                        pe.wait_ge(q_stacked[q], i * 64 + 64)
                    b, t0 = q // QUAD, 2 * (q % QUAD)
                    pe.wait_ge(sc_free, quad(j, q))
                    bank = sc_bank(q)
                    for h in range(QUAD):
                        t, parity = t0 + h // 2, h % 2
                        for part in (HI, LO):
                            mm = pe.matmul(bank[:, tile(h)], q_stack[:, parity, t, tok(b)],
                                           k_stack[:, part, parity, t, tok(b)], start=(part == HI), stop=(part == LO))
                    mm.then_inc(sc_full, 1)

                def exp_transpose(q):
                    pe.wait_ge(exp_ready, quad(j, q))
                    pe.wait_ge(et_free, quad(j, q))
                    for h in range(QUAD):
                        mm = pe.transpose(et_bank(q)[:, tile(h)], expd[:, q % 2, h, :], ident)
                    mm.then_inc(et_full, 1)

                def back_begin(name):
                    k = BACK.index(name)
                    pe.wait_ge(bj_free, bj(j, name))
                    return bj_bank(k)

                def weigh(q):
                    b = q // QUAD
                    pe.wait_ge(exp_split, quad(j, q) + FREE)
                    if q % QUAD == 0:
                        pe.wait_ge(kv_split, kv(j, (J_VV1, J_VV3)[b]) + FREE)
                    bank = back_begin(f"pv{q}")
                    for h in range(QUAD):
                        head = QUAD * (q % QUAD) + h
                        mm = split_products(pe, bank[:, h * VW:(h + 1) * VW], hilo(exp_t[:, q % 2], h),
                                            hilo(v_nat, b, head))
                    mm.then_inc(bj_full, 1)

                def heads_transpose(c):
                    pe.wait_ge(bj_free, bj(j, f"pv{2 * c + 1}") + FREE)
                    bank = back_begin(f"ct{c}")
                    for t in range(4):
                        mm = pe.transpose(bank[:, tile(t)], heads_out[:, c % 2, tile(t)], ident)
                    mm.then_inc(bj_full, 1)

                def output(b):
                    pe.wait_ge(bj_free, bj(j, f"ct{2 * b + 1}") + FREE)
                    bank = back_begin(f"out{b}")
                    for kt in range(ET):
                        mm = split_products(pe, bank[:, 0:D], hilo(heads_t, kt), hilo(keep["cross_Wo"], kt),
                                            first=(kt == 0), last=(kt == ET - 1))
                    mm.then_inc(bj_full, 1)

                if back:
                    queries(1)
                if front:
                    keys(0)
                if back:
                    queries(2)
                    score(0)
                    queries(3)
                    score(1)
                if front:
                    keys(1)
                if back:
                    score(2)
                    exp_transpose(0)
                if front:
                    keys(2)
                if back:
                    score(3)
                    exp_transpose(1)
                    weigh(0)
                if front:
                    keys(3)
                if back:
                    score(4)
                    exp_transpose(2)
                    weigh(1)
                    score(5)
                    exp_transpose(3)
                if front:
                    values(0)
                if back:
                    weigh(2)
                if ahead:
                    x_transpose()
                if back:
                    heads_transpose(0)
                    score(6)
                    exp_transpose(4)
                    weigh(3)
                if ahead:
                    fold_query()
                if back:
                    heads_transpose(1)
                    score(7)
                    exp_transpose(5)
                    weigh(4)
                if front:
                    probs_transpose(0)
                    values(1)
                    probs_transpose(1)
                if back:
                    exp_transpose(6)
                    weigh(5)
                    output(0)
                if front:
                    attend()
                if back:
                    exp_transpose(7)
                    weigh(6)
                if ahead:
                    fold_value(0)
                if back:
                    heads_transpose(2)
                if ahead:
                    fold_value(1)
                if back:
                    weigh(7)
                if front:
                    values(2)
                if ahead:
                    raw_scores()
                if front:
                    x1_transpose()
                if back:
                    heads_transpose(3)
                if front:
                    values(3)
                    queries(0)
                if ahead:
                    context_transpose()
                if back:
                    output(1)

            body(-1, False, False, True)
            body(0, True, False, True)
            with pe.Fori(1, PAIRS - 1) as i:
                body(i, True, True, True)
            body(PAIRS - 1, True, True, False)
            body(PAIRS, False, True, False)

        @block.scalar
        def _(act):
            def body(i, front, back, ahead):
                j = i - 1

                def hi(k):
                    act.wait_ge(fj_full, fj(i, k))
                    if k == J_K0 and back:
                        act.wait_ge(k_stacked, i * 128)
                    if k in J_Q:
                        act.wait_ge(q_stacked[(J_Q.index(k) + 2) % 4], i * 64 if k == J_Q1 else (i + 1) * 64)
                    if k == J_G:
                        for t in range(DT):
                            op = act.activation(g_t[:, HI, t, :], fj_bank(k)[:, t * 2 * P:(t + 1) * 2 * P],
                                                ACT.Identity, bias=keep["g_bias"][:, t:t + 1])
                    else:
                        dst, at, src = landing(k)
                        op = act.activation(hilo(dst, *at)[HI], src, ACT.Copy)
                    if k in KV:
                        act.wait_ge(kv_split, kv(i, k))
                        act.activation(kv_copy[:, KV.index(k) % 2, :], fj_bank(k), ACT.Copy).then_inc(
                            fj_free[k % 2], steps(k, same_bank(k), front, back, ahead))
                        return
                    op.then_inc(fj_hi, steps(k, WITH_HI, front, back, ahead))

                def exponential(q):
                    act.wait_ge(scores_ready, quad(j, q))
                    for h in range(QUAD):
                        op = act.activation(expd[:, q % 2, h, :], scores[:, q % 2, h, :], ACT.Exp,
                                            bias=neg_max[:, q % 2, h:h + 1])
                    op.then_inc(exp_ready, 1)

                def exp_hi(q):
                    act.wait_ge(et_full, quad(j, q))
                    act.activation(exp_t[:, q % 2, HI], et_bank(q).rearrange("p (h s) -> p h s", h=QUAD), ACT.Copy)
                    act.wait_ge(exp_split, quad(j, q))
                    act.activation(exp_copy[:, q % 2], et_bank(q).rearrange("p (h s) -> p h s", h=QUAD),
                                   ACT.Copy).then_inc(et_free, 1)

                def heads_hi(c):
                    act.wait_ge(bj_full, bj(j, f"ct{c}"))
                    act.activation(heads_t[:, HI, 4 * (c % 2):4 * (c % 2) + 4, :],
                                   bj_bank(BACK.index(f"ct{c}")).rearrange("p (t s) -> p t s", t=4),
                                   ACT.Copy).then_inc(bj_hi, 1)

                def self_softmax():
                    act.wait_ge(softmax_in, i + 1)
                    for b in range(2):
                        for k, (src, dst, scale) in enumerate(((win_in, win_e, 1.0), (sparse_in, sparse_e, 1.0),
                                                               (comp_in, comp_e, 1.0 / GROUP))):
                            op = act.activation(dst[:, b, :], src[:, b, :], ACT.Exp, bias=neg_maxes[:, b, k:k + 1],
                                                scale=scale, accum_out=sums[:, b, k:k + 1])
                    op.then_inc(softmax_exp, 1)

                if back:
                    hi(J_Q1)
                if front:
                    hi(J_K0)
                if back:
                    hi(J_Q2)
                    exponential(0)
                    hi(J_Q3)
                    exponential(1)
                if front:
                    hi(J_K1)
                if back:
                    exp_hi(0)
                    exponential(2)
                if front:
                    hi(J_K2)
                if back:
                    exp_hi(1)
                    exponential(3)
                if front:
                    hi(J_K3)
                if back:
                    exp_hi(2)
                    exponential(4)
                    exp_hi(3)
                    exponential(5)
                if front:
                    hi(J_VV0)
                if ahead:
                    hi(J_X)
                if back:
                    heads_hi(0)
                    exp_hi(4)
                if front:
                    self_softmax()
                if back:
                    exponential(6)
                if ahead:
                    hi(J_G)
                if back:
                    heads_hi(1)
                    exp_hi(5)
                if front:
                    hi(J_PT0)
                if back:
                    exponential(7)
                if front:
                    hi(J_VV1)
                    hi(J_PT1)
                if back:
                    exp_hi(6)
                    exp_hi(7)
                if ahead:
                    hi(J_V0)
                if back:
                    heads_hi(2)
                if ahead:
                    hi(J_V1)
                if front:
                    hi(J_VV2)
                    hi(J_X1)
                if back:
                    heads_hi(3)
                if front:
                    hi(J_VV3)
                    hi(J_Q0)
                if ahead:
                    hi(J_CTX)

            body(-1, False, False, True)
            body(0, True, False, True)
            with act.Fori(1, PAIRS - 1) as i:
                body(i, True, True, True)
            body(PAIRS - 1, True, True, False)
            body(PAIRS, False, True, False)

        @block.vector
        def _(dve):
            dve.memset(v_nat[:, HI, :, :, DH:DH + 1], 1.0)
            dve.memset(v_nat[:, HI, :, :, DH + 1:VW], 0.0)
            dve.memset(v_nat[:, LO, :, :, DH:VW], 0.0)
            for n in range(2):
                dve.memset(start[:, 10 * n:10 * n + 1], 0.0).then_inc(fj_free[n], 1)
            dve.memset(start[:, 1:2], 0.0).then_inc(sc_free, FREE)
            dve.memset(start[:, 11:12], 0.0).then_inc(exp_split, FREE)
            dve.memset(start[:, 12:13], 0.0).then_inc(kv_split, FREE)
            dve.memset(start[:, 2:3], 0.0).then_inc(et_free, FREE)
            dve.memset(start[:, 3:4], 0.0).then_inc(bj_free, FREE)
            for b in range(2):
                dve.memset(start[:, 4 + b:5 + b], 0.0).then_inc(x2_free[b], 16)
            for n in range(4):
                dve.memset(start[:, 6 + n:7 + n], 0.0).then_inc(q_stacked[n], 64)

            def body(i, front, back, ahead):
                j = i - 1

                def lo(k):
                    dve.wait_ge(fj_hi, fj_his(i, k))
                    if k == J_G:
                        for t in range(DT):
                            op = dve.scalar_tensor_tensor(g_t[:, LO, t, :], fj_bank(k)[:, t * 2 * P:(t + 1) * 2 * P],
                                                          keep["g_bias"][:, t:t + 1], g_t[:, HI, t, :].bitcast(F32),
                                                          ALU.add, ALU.subtract)
                    else:
                        dst, at, src = landing(k)
                        hi = hilo(dst, *at)[HI]
                        hi = hi.bitcast(F32) if dst.dtype == F32R else hi
                        if k in (J_V0, J_V1):
                            b = int(k == J_V1)
                            dve.tensor_scalar(row_rq[:, b:b + 1], fj_bank(k)[:, D:D + 1],
                                              keep["qk_bias"][:], None, ALU.add).then_inc(rq_ready, 1)
                        op = dve.tensor_tensor(hilo(dst, *at)[LO], src, hi, ALU.subtract)
                    op.then_inc(fj_free[k % 2], steps(k, same_bank(k), front, back, ahead))

                def statistics(n, src, st, stats_done, mom, moments_done):
                    if src is x1:
                        wait_apart(dve, fj_free[J_AO % 2], fj_left(n, J_AO))
                    for b in range(2):
                        op = dve.bn_stats(st[:, b, :], src[:, b, :])
                    op.then_inc(stats_done, 1)
                    wait_apart(dve, stats_done, n + 1)
                    for b in range(2):
                        op = dve.bn_aggr(mom[:, b, :], st[:, b, :])
                    op.then_inc(moments_done, 1)

                def normalise(n, src, mom, rs, rstd_done, dst, done):
                    dve.wait_ge(rstd_done, n + 1)
                    for b in range(2):
                        op = dve.tensor_scalar(dst[:, b, :], src[:, b, :], mom[:, b, 0:1], rs[:, b:b + 1],
                                               ALU.subtract, ALU.mult)
                    op.then_inc(done, 1)

                def add_mask(q):
                    b = q // QUAD
                    if q % QUAD == 0:
                        wait_apart(dve, mask_loaded[b], 16 * (j + 1))
                    if q >= 2:
                        wait_apart(dve, exp_ready, quad(j, q - 2))
                    wait_apart(dve, sc_full, quad(j, q))
                    for h in range(QUAD):
                        op = dve.tensor_tensor_reduce(scores[:, q % 2, h, :], sc_bank(q)[:, tile(h)], mask[:, b, :],
                                                      1.0, NEG, ALU.add, ALU.max, score_max[:, q % 2, h:h + 1])
                    op.then_inc(sc_free, 1)

                def negate_max(q):
                    dve.wait_ge(sc_free, quad(j, q) + FREE)
                    dve.tensor_scalar(neg_max[:, q % 2, :], score_max[:, q % 2, :], -1.0, None,
                                      ALU.mult).then_inc(scores_ready, 1)

                def mask_scores(q):
                    add_mask(q)
                    negate_max(q)

                def pv_view(q):
                    return bj_bank(BACK.index(f"pv{q}"))[:, 0:QUAD * VW].rearrange("p (h w) -> p h w", w=VW)

                def row_sums(q):
                    dve.wait_ge(bj_full, bj(j, f"pv{q}"))
                    dve.reciprocal(inv_den[:, q % 2, :], pv_view(q)[:, :, DH]).then_inc(den_ready, 1)

                def divide(q):
                    dve.wait_ge(den_ready, quad(j, q))
                    at = slice((q % 2) * QUAD * DH, (q % 2 + 1) * QUAD * DH)
                    dve.tensor_tensor(heads_out[:, (q // 2) % 2, at].rearrange("p (h d) -> p h d", d=DH),
                                      pv_view(q)[:, :, 0:DH], inv_den[:, q % 2, :].unsqueeze(2).to_broadcast([P, QUAD, DH]),
                                      ALU.mult).then_inc(bj_free, 1)

                def heads_lo(c):
                    dve.wait_ge(bj_hi, bj_his(j, c))
                    at = slice(4 * (c % 2), 4 * (c % 2) + 4)
                    dve.tensor_tensor(heads_t[:, LO, at, :], bj_bank(BACK.index(f"ct{c}")).rearrange("p (t s) -> p t s", t=4),
                                      heads_t[:, HI, at, :].bitcast(F32), ALU.subtract).then_inc(bj_free, 1)

                def raw_scores():
                    dve.wait_ge(rq_ready, i * 2 + 4)
                    dve.wait_ge(fj_full, fj(i, J_RAW))
                    for b in range(2):
                        at = b * 2 * P + b * P
                        op = dve.tensor_scalar(raw[:, b, :], fj_bank(J_RAW)[:, at:at + P], row_rq[:, b:b + 1],
                                               1.0 / 16.0, ALU.add, ALU.mult)
                    op.then_inc(fj_free[J_RAW % 2], steps(J_RAW, same_bank(J_RAW), front, back, ahead))

                def top_round(n, r):
                    for b in range(2):
                        if r == 0:
                            wait_apart(dve, fj_free[J_RAW % 2], fj_left(n - 1, J_RAW))
                        else:
                            wait_apart(dve, top_out, n * 16 + (2 * (r - 1) + b + 1))
                        dve.max(top8[:, b, :], (raw if r == 0 else left)[:, b, :]).then_inc(top_found, 1)
                    for b in range(2):
                        wait_apart(dve, top_found, n * 16 + (2 * r + b + 1))
                        dve.match_replace(left[:, b, :], top8[:, b, :], (raw if r == 0 else left)[:, b, :],
                                          NEG).then_inc(top_out, 1)

                def window_and_compressed(n):
                    wait_apart(dve, fj_free[J_RAW % 2], fj_left(n - 1, J_RAW))
                    for b in range(2):
                        dve.tensor_tensor_reduce(win_in[:, b, :], raw[:, b, :], keep["causal"][:], 1.0, NEG,
                                                 ALU.add, ALU.max, maxes[:, b, 0:1])
                    dve.tensor_reduce(comp_in[:], raw[:].rearrange("p b (g f) -> p b g f", f=GROUP), AX,
                                      ALU.add).then_inc(comp_ready, 1)
                    dve.wait_ge(comp_ready, n + 1)
                    dve.tensor_reduce(maxes[:, :, 2], comp_in[:], AX, ALU.max)

                def sparse():
                    dve.wait_ge(top_out, i * 16 + 16)
                    dve.scalar_tensor_tensor(sparse_in[:], left[:], NEG, raw[:], ALU.is_equal,
                                             ALU.mult).then_inc(sparse_ready, 1)
                    dve.wait_ge(sparse_ready, i + 1)
                    dve.tensor_reduce(maxes[:, :, 1], sparse_in[:], AX, ALU.max).then_inc(max_ready, 1)
                    dve.wait_ge(max_ready, i + 1)
                    dve.tensor_tensor(neg_maxes[:], maxes[:], keep["negs"][:], ALU.mult).then_inc(softmax_in, 1)

                def mix():
                    dve.wait_ge(softmax_exp, i + 1)
                    dve.reciprocal(inv_sums[:], sums[:]).then_inc(inv_ready, 1)
                    dve.wait_ge(inv_ready, i + 1)
                    dve.tensor_tensor(weights[:], inv_sums[:], keep["third"][:], ALU.mult).then_inc(weights_ready, 1)
                    dve.wait_ge(weights_ready, i + 1)
                    for b in range(2):
                        dve.tensor_scalar(win_e[:, b, :], win_e[:, b, :], weights[:, b, 0:1], None,
                                          ALU.mult).then_inc(mix_a_ready, 1)
                    for b in range(2):
                        dve.wait_ge(mix_a_ready, i * 2 + (b + 1))
                        dve.scalar_tensor_tensor(sparse_e[:, b, :], sparse_e[:, b, :], weights[:, b, 1:2], win_e[:, b, :],
                                                 ALU.mult, ALU.add).then_inc(mix_b_ready, 1)
                    for b in range(2):
                        dve.wait_ge(mix_b_ready, i * 2 + (b + 1))
                        dve.scalar_tensor_tensor(probs[:, b, :].rearrange("p (g f) -> p g f", f=GROUP),
                                                 comp_e[:, b, :].unsqueeze(2).to_broadcast([P, P // GROUP, GROUP]),
                                                 weights[:, b, 2:3], sparse_e[:, b, :].rearrange("p (g f) -> p g f", f=GROUP),
                                                 ALU.mult, ALU.add).then_inc(probs_ready, 1)

                def first_residual():
                    dve.wait_ge(x_bias_ready, i + 1)
                    if back:
                        dve.wait_ge(x1_kept, i)
                    dve.wait_ge(fj_full, fj(i, J_AO))
                    dve.tensor_tensor(x1[:].rearrange("p b d -> p (b d)"), fj_bank(J_AO),
                                      x_bias[:].rearrange("p b d -> p (b d)"),
                                      ALU.add).then_inc(fj_free[J_AO % 2], steps(J_AO, same_bank(J_AO), front, back, ahead))

                def second_residual(b):
                    dve.wait_ge(bj_full, bj(j, f"out{b}"))
                    dve.wait_ge(x2_free[b], 16 * (j + 1))
                    dve.wait_ge(x1_kept, j + 1)
                    dve.tensor_tensor(x2[:, b, :], bj_bank(BACK.index(f"out{b}"))[:, 0:D],
                                      x1_old[:, b, :], ALU.add).then_inc(bj_free, 1)

                if back:
                    lo(J_Q1)
                if front:
                    top_round(i, 1)
                if back:
                    lo(J_Q2)
                    mask_scores(0)
                if front:
                    top_round(i, 2)
                if back:
                    lo(J_Q3)
                    mask_scores(1)
                if front:
                    top_round(i, 3)
                if back:
                    mask_scores(2)
                if front:
                    top_round(i, 4)
                if back:
                    mask_scores(3)
                    row_sums(0)
                    divide(0)
                if ahead:
                    dve.wait_ge(x_loaded, 16 * (i + 2))
                    statistics(i + 1, x_in, stats, stats_x, moments, moments_x)
                if front:
                    top_round(i, 5)
                if back:
                    mask_scores(4)
                    row_sums(1)
                    divide(1)
                if ahead:
                    normalise(i + 1, x_in, moments, rstd, rstd_x, xn, xn_ready)
                if front:
                    top_round(i, 6)
                if back:
                    mask_scores(5)
                if front:
                    top_round(i, 7)
                    sparse()
                if back:
                    row_sums(2)
                    divide(2)
                if ahead:
                    lo(J_X)
                if back:
                    mask_scores(6)
                    heads_lo(0)
                    row_sums(3)
                    divide(3)
                if front:
                    mix()
                if ahead:
                    lo(J_G)
                if back:
                    mask_scores(7)
                    heads_lo(1)
                if front:
                    lo(J_PT0)
                if back:
                    row_sums(4)
                    divide(4)
                if front:
                    lo(J_PT1)
                if back:
                    row_sums(5)
                    divide(5)
                    second_residual(0)
                if front:
                    first_residual()
                if back:
                    row_sums(6)
                if front:
                    statistics(i, x1, stats1, stats_x1, moments1, moments_x1)
                if back:
                    divide(6)
                if ahead:
                    lo(J_V0)
                if back:
                    heads_lo(2)
                if ahead:
                    lo(J_V1)
                if back:
                    row_sums(7)
                if front:
                    normalise(i, x1, moments1, rstd1, rstd_x1, xn1, xn1_ready)
                if back:
                    divide(7)
                if ahead:
                    raw_scores()
                if front:
                    lo(J_X1)
                if back:
                    heads_lo(3)
                if front:
                    lo(J_Q0)
                if ahead:
                    top_round(i + 1, 0)
                    lo(J_CTX)
                    window_and_compressed(i + 1)
                if back:
                    second_residual(1)

            body(-1, False, False, True)
            body(0, True, False, True)
            with dve.Fori(1, PAIRS - 1) as i:
                body(i, True, True, True)
            body(PAIRS - 1, True, True, False)
            body(PAIRS, False, True, False)


def feed_forward(nc, keep, psum, x2_dram, out_dram):
    with ExitStack() as ctx:
        def sb(name, shape, dt=F32):
            return ctx.enter_context(nc.sbuf_tensor(name, shape, dt))

        def sem(name):
            return ctx.enter_context(nc.semaphore(name))

        GB = 4
        GROUPS = NB // GB
        TOK = GB * P
        LAG = 4
        RING = 4
        TURN = 4

        normed = sb("normed", [P, NB, D])
        xq_t = sb("xq_t", [P, DT, NB * P], BF16)
        x_load = sb("x_load", [P, TURN, GB, D])
        stats = sb("f_stats", [P, TURN, GB, 6])
        moments = sb("f_moments", [P, TURN, GB, 2])
        var_eps = sb("f_var_eps", [P, GB])
        rstd = sb("f_rstd", [P, TURN, GB])
        scaled_mean = sb("scaled_mean", [P, GB])
        shift = sb("shift", [P, TURN, GB])
        row_max = sb("row_max", [P, NB])
        tile_max = sb("tile_max", [P, GROUPS * ET])
        peak = sb("peak", [P, 4])
        scale = sb("act_scale", [P, 2])
        inv_scale = sb("inv_scale", [P, 2])
        both = sb("both_scales", [P, 2])
        b1_scaled = sb("b1_scaled", [P, ET])
        b2_scaled = sb("b2_scaled", [P, D])
        rounded = sb("rounded", [P, 2, GB * D])
        xq = sb("xq", [P, 2, GB * D], BF16)
        start = sb("f_start", [P, 9])
        ident16 = sb("ident16", [P, P], BF16)
        hidden = sb("hidden", [P, RING, TOK])
        h_round = sb("h_round", [P, RING, TOK])
        h_q = sb("h_q", [P, ET, TOK], BF16)
        x_again = sb("x_again", [P, 2, GB, D])
        result = sb("result", [P, 2, GB, D])

        loaded = [sem(f"f_loaded{n}") for n in range(TURN)]
        stats_done, moments_done, eps_done, rstd_done, mean_done, shift_done = (
            sem(n) for n in ("f_stats_done", "f_moments_done", "f_eps_done", "f_rstd_done", "f_mean_done", "f_shift_done"))
        norm_done, max_done = sem("f_norm_done"), sem("f_max_done")
        peak_own, peak_all, scale_step, scales_done = sem("peak_own"), sem("peak_all"), sem("f_scale_step"), sem("scales_done")
        xq_rounded, xq_ready, xt_full, xt_done = sem("xq_rounded"), sem("xq_ready"), sem("xt_full"), sem("xt_done")
        ident_done = sem("ident_done")
        u_full, h_ready, h_seen = sem("u_full"), sem("h_ready"), sem("h_seen")
        u2_full, h2_ready, h2_rounded, hq_ready = sem("u2_full"), sem("h2_ready"), sem("h2_rounded"), sem("hq_ready")
        acc_step, acc_full, acc_free = sem("acc_step"), sem("acc_full"), sem("acc_free")
        again_loaded = [sem("again_loaded0"), sem("again_loaded1")]
        bias_added = sem("bias_added")
        stored = [sem("stored0"), sem("stored1")]

        x2_groups = x2_dram.rearrange("(g b) s d -> g s b d", b=GB)
        out_groups = out_dram.rearrange("(g b) s d -> g s b d", b=GB)
        u_bank = lambda t: psum[:, t % RING, :]
        xt_bank = psum[:, 4, :].bitcast(BF16)

        block = ctx.enter_context(nc.Block())

        @block.sync
        def _(sp):
            def load(g, side):
                sp.dma_start(x_load[:, side], x2_groups[g]).then_inc(loaded[side], 16)

            for n in range(TURN):
                load(n, n)
            with sp.Fori(1, GROUPS // TURN) as turn:
                for n in range(TURN):
                    wait_apart(sp, norm_done, turn * TURN + (n + 1 - TURN))
                    load(turn * TURN + n, n)

            def reload(n, side):
                sp.dma_start(x_again[:, side], x2_groups[n]).then_inc(again_loaded[side], 16)

            reload(0, 0)
            reload(1, 1)

            def store(n, side):
                wait_apart(sp, acc_free, GB * (n + 2))
                sp.dma_start(out_groups[n], result[:, side]).then_inc(stored[side], 16)

            with sp.Fori(0, GROUPS // 2 - 1) as h:
                for side in range(2):
                    store(h * 2 + side, side)
                    reload(h * 2 + side + 2, side)
            for side in range(2):
                store(GROUPS - 2 + side, side)
            for side in range(2):
                wait_apart(sp, stored[side], 16 * (GROUPS // 2 + 1))

        @block.gpsimd
        def _(pool):
            with pool.Fori(0, GROUPS // TURN) as turn:
                for side in range(TURN):
                    g = turn * TURN + side
                    wait_apart(pool, moments_done, g + 1)
                    pool.tensor_scalar(var_eps[:], moments[:, side, :, 1], EPS, None, ALU.add).then_inc(eps_done, 1)
                    pool.wait_ge(eps_done, g + 1)
                    pool.tensor_tensor(rstd[:, side], var_eps[:], keep["half4"][:], ALU.pow).then_inc(rstd_done, 1)
                    pool.wait_ge(rstd_done, g + 1)
                    pool.tensor_tensor(scaled_mean[:], moments[:, side, :, 0], rstd[:, side], ALU.mult).then_inc(mean_done, 1)
                    wait_apart(pool, mean_done, g + 1)
                    pool.tensor_scalar(shift[:, side], scaled_mean[:], -1.0, None, ALU.mult).then_inc(shift_done, 1)

            def largest(k):
                pool.wait_ge(peak_own, k + 1)
                pool.partition_all_reduce(peak[:, 2 * k + 1:2 * k + 2], peak[:, 2 * k:2 * k + 1], P,
                                          RMAX).then_inc(peak_all, 1)

            largest(0)
            with pool.Fori(0, GROUPS // 2) as h:
                for side in range(2):
                    g = h * 2 + side
                    wait_apart(pool, xt_full, g + 1)
                    wait_apart(pool, xq_rounded, g + 1)
                    pool.tensor_scalar(xq[:, side], rounded[:, side], MAGIC, None, ALU.subtract).then_inc(xq_ready, 1)
            largest(1)

            pool.wait_ge(scales_done, 2)
            with pool.Fori(0, GROUPS // 2) as h:
                for side in range(2):
                    pool.wait_ge(again_loaded[side], h * 16 + 16)
                    for b in range(GB):
                        op = pool.tensor_tensor(x_again[:, side, b, :], x_again[:, side, b, :], b2_scaled[:], ALU.add)
                    op.then_inc(bias_added, 1)

        def hidden_tile(pe, g, t, full):
            for kt in range(DT):
                mm = pe.matmul(u_bank(t), keep["w1_q"][:, kt, t * P:(t + 1) * P], xq_t[:, kt, bass.ts(g, TOK)],
                               start=(kt == 0), stop=(kt == DT - 1))
            mm.then_inc(full, 1)

        @block.tensor
        def _(pe):
            def x_transpose(g, side):
                pe.wait_ge(xq_ready, g + 1)
                pe.wait_ge(xt_done, g + 1)
                for dt in range(DT):
                    for b in range(GB):
                        mm = pe.transpose(xt_bank[:, (dt * GB + b) * P:(dt * GB + b + 1) * P],
                                          xq[:, side, b * D + dt * P:b * D + (dt + 1) * P], ident16[:])
                mm.then_inc(xt_full, 1)

            def first_pass(g, side, ahead):
                pe.wait_ge(xt_done, g + 2)
                for t in range(ET):
                    pe.wait_ge(h_ready, g * ET + (t + 1))
                    hidden_tile(pe, g, t, u_full)
                    if t == 5 and ahead:
                        x_transpose(g + 1, 1 - side)

            pe.wait_ge(ident_done, 1)
            x_transpose(0, 0)
            with pe.Fori(0, GROUPS // 2 - 1) as h:
                for side in range(2):
                    first_pass(h * 2 + side, side, True)
            first_pass(GROUPS - 2, 0, True)
            first_pass(GROUPS - 1, 1, False)

            def second_layer(g, n_tile, t):
                pe.wait_ge(hq_ready, n_tile)
                for b in range(GB):
                    if t == 0:
                        pe.wait_ge(acc_free, g * GB + (b + 1))
                    mm = pe.matmul(psum[:, 4 + b, 0:D], h_q[:, t, b * P:(b + 1) * P], keep["w2_q"][:, t, :],
                                   start=(t == 0), stop=(t == ET - 1))
                    if t == ET - 1:
                        mm.then_inc(acc_full, 1)
                if t < ET - 1:
                    mm.then_inc(acc_step, 1)

            def group(g, before, now):
                for t in range(ET):
                    if now:
                        pe.wait_ge(h2_ready, g * ET + (t + 1))
                        hidden_tile(pe, g, t, u2_full)
                    if t < LAG and before:
                        second_layer(g - 1, g * ET + (t - LAG + 1), ET - LAG + t)
                    if t >= LAG and now:
                        second_layer(g, g * ET + (t - LAG + 1), t - LAG)

            pe.wait_ge(h_ready, GROUPS * ET + RING)
            group(0, False, True)
            with pe.Fori(1, GROUPS) as g:
                group(g, True, True)
            group(GROUPS, True, False)

        @block.scalar
        def _(act):
            with act.Fori(0, GROUPS // TURN) as turn:
                for side in range(TURN):
                    g = turn * TURN + side
                    act.wait_ge(shift_done, g + 1)
                    for b in range(GB):
                        op = act.activation(normed[:, bass.ds(g * GB + b, 1), :].rearrange("p b d -> p (b d)"),
                                            x_load[:, side, b, :], ACT.Identity,
                                            bias=shift[:, side, b:b + 1], scale=rstd[:, side, b:b + 1])
                    op.then_inc(norm_done, 1)

            def gelus(full, used, ready):
                with act.Fori(0, GROUPS // TURN) as turn:
                    for n in range(TURN * ET):
                        act.wait_ge(full, turn * (TURN * ET) + (n + 1))
                        act.wait_ge(used, turn * (TURN * ET) + (n + 1))
                        act.activation(hidden[:, n % RING, :], u_bank(n), ACT.Gelu, bias=b1_scaled[:, n % ET:n % ET + 1],
                                       scale=both[:, 0:1]).then_inc(ready, 1)

            act.wait_ge(scales_done, 1)
            gelus(u_full, h_seen, h_ready)
            act.wait_ge(h_seen, GROUPS * ET + RING)
            gelus(u2_full, h2_rounded, h2_ready)

        @block.vector
        def _(dve):
            dve.memset(start[:, 0:1], 0.0).then_inc(h_ready, RING)
            dve.memset(start[:, 1:2], 0.0).then_inc(h2_ready, RING)
            dve.memset(start[:, 2:3], 0.0).then_inc(h_seen, RING)
            dve.memset(start[:, 3:4], 0.0).then_inc(h2_rounded, RING)
            dve.memset(start[:, 4:5], 0.0).then_inc(acc_free, GB)
            for side in range(2):
                dve.memset(start[:, 5 + side:6 + side], 0.0).then_inc(stored[side], 16)
            dve.memset(start[:, 7:8], 0.0).then_inc(xt_full, 2)
            dve.memset(start[:, 8:9], 0.0).then_inc(xt_done, 1)
            dve.tensor_copy(ident16[:], keep["ident"][:]).then_inc(ident_done, 1)

            def token_moments(g, side, turn):
                dve.wait_ge(loaded[side], turn * 16 + 16)
                for b in range(GB):
                    op = dve.bn_stats(stats[:, side, b, :], x_load[:, side, b, :])
                op.then_inc(stats_done, 1)
                wait_apart(dve, stats_done, g + 1)
                for b in range(GB):
                    op = dve.bn_aggr(moments[:, side, b, :], stats[:, side, b, :])
                op.then_inc(moments_done, 1)

            def largest_normed(g):
                dve.wait_ge(norm_done, g + 1)
                dve.tensor_reduce(row_max[:, bass.ts(g, GB)], normed[:, bass.ts(g, GB), :], AX, ALU.max,
                                  apply_absolute_value=True).then_inc(max_done, 1)

            for n in range(TURN):
                if n >= 2:
                    largest_normed(n - 2)
                token_moments(n, n, 0)
            with dve.Fori(1, GROUPS // TURN) as turn:
                for n in range(TURN):
                    largest_normed(turn * TURN + (n - 2))
                    token_moments(turn * TURN + n, n, turn)
            largest_normed(GROUPS - 2)
            largest_normed(GROUPS - 1)

            def activation_scale(k, maxima):
                dve.tensor_reduce(peak[:, 2 * k:2 * k + 1], maxima, AX, ALU.max).then_inc(peak_own, 1)
                dve.wait_ge(peak_all, k + 1)
                dve.tensor_scalar(scale[:, k:k + 1], peak[:, 2 * k + 1:2 * k + 2], MIN_RANGE, 1.0 / QP,
                                  ALU.max, ALU.mult).then_inc(scale_step, 1)
                dve.wait_ge(scale_step, 2 * k + 1)
                dve.reciprocal(inv_scale[:, k:k + 1], scale[:, k:k + 1])
                dve.tensor_tensor(both[:, k:k + 1], scale[:, k:k + 1], keep["w_scale"][:, k:k + 1],
                                  ALU.mult).then_inc(scale_step, 1)
                dve.wait_ge(scale_step, 2 * k + 2)
                out, bias = ((b1_scaled, keep["b1_col"]), (b2_scaled, keep["b2_row"]))[k]
                dve.tensor_scalar(out[:], bias[:], both[:, k:k + 1], None, ALU.mult).then_inc(scales_done, 1)

            dve.wait_ge(max_done, GROUPS)
            activation_scale(0, row_max[:])

            def copy_x(g):
                dve.wait_ge(xt_full, g + 3)
                dve.tensor_copy(xq_t[:, :, bass.ts(g, TOK)],
                                xt_bank.rearrange("p (t s) -> p t s", t=DT)).then_inc(xt_done, 1)

            def round_x(g, side):
                dve.tensor_scalar(rounded[:, side], normed[:, bass.ts(g, GB), :].rearrange("p b d -> p (b d)"),
                                  inv_scale[:, 0:1], MAGIC, ALU.mult, ALU.add).then_inc(xq_rounded, 1)

            def first_pass(g, side, ahead, further):
                for t in range(ET):
                    if t == 6 and further:
                        round_x(g + 2, side)
                    dve.wait_ge(h_ready, g * ET + (t + 1) + RING)
                    dve.tensor_reduce(tile_max[:, bass.ds(g * ET + t, 1)], hidden[:, t % RING, :], AX, ALU.max,
                                      apply_absolute_value=True).then_inc(h_seen, 1)
                    if t == 5 and ahead:
                        copy_x(g + 1)

            round_x(0, 0)
            round_x(1, 1)
            copy_x(0)
            with dve.Fori(0, GROUPS // 2 - 1) as h:
                for side in range(2):
                    first_pass(h * 2 + side, side, True, True)
            first_pass(GROUPS - 2, 0, True, False)
            first_pass(GROUPS - 1, 1, False, False)

            dve.wait_ge(h_seen, GROUPS * ET + RING)
            activation_scale(1, tile_max[:])

            def add_residual(n, side, turn):
                dve.wait_ge(bias_added, n + 1)
                dve.wait_ge(stored[side], turn * 16 + 16)
                for b in range(GB):
                    dve.wait_ge(acc_full, n * GB + (b + 1))
                    dve.scalar_tensor_tensor(result[:, side, b, :], psum[:, 4 + b, 0:D], both[:, 1:2],
                                             x_again[:, side, b, :], ALU.mult, ALU.add).then_inc(acc_free, 1)

            def round_up(g, t, before):
                if before or t >= RING:
                    dve.wait_ge(hq_ready, g * ET + (t + 1 - RING))
                dve.wait_ge(h2_ready, g * ET + (t + 1) + RING)
                dve.tensor_scalar(h_round[:, t % RING, :], hidden[:, t % RING, :], inv_scale[:, 1:2], MAGIC,
                                  ALU.mult, ALU.add).then_inc(h2_rounded, 1)

            def take_magic_off(g, t, before):
                if before and t == ET - 1:
                    dve.wait_ge(acc_full, g * GB)
                elif before:
                    dve.wait_ge(acc_step, (g - 1) * (ET - 1) + (t + 1))
                dve.wait_ge(h2_rounded, g * ET + (t + 1) + RING)
                dve.tensor_scalar(h_q[:, t, :], h_round[:, t % RING, :], MAGIC, None, ALU.subtract).then_inc(hq_ready, 1)

            def group(g, side, turn, before, now, far=True):
                for t in range(ET):
                    if before and t == LAG:
                        add_residual(g - 1, side, turn)
                    if now:
                        round_up(g, t, before)
                        if t > 0:
                            take_magic_off(g, t - 1, before)
                    if before and t == 0:
                        take_magic_off(g - 1, ET - 1, far)

            group(0, 0, 0, False, True)
            group(1, 0, 0, True, True, False)
            with dve.Fori(1, GROUPS // 2) as h:
                group(h * 2, 1, h - 1, True, True)
                group(h * 2 + 1, 0, h, True, True)
            group(GROUPS, 1, GROUPS // 2 - 1, True, False)


def decoder_layer(nc, dram, out_dram):
    with ExitStack() as ctx:
        def sb(name, shape, dt=F32):
            return ctx.enter_context(nc.sbuf_tensor(name, shape, dt))

        x2_dram = nc.dram_tensor("x2_residual", (NB, P, D), F32, kind="Internal").ap()
        psum = ctx.enter_context(nc.psum_tensor("banks", [P, 8, 512], F32))
        keep = {
            "ident": sb("ident", [P, P]),
            "w1_q": sb("w1_q", [P, DT, INNER], BF16),
            "w2_q": sb("w2_q", [P, ET, D], BF16),
            "w_scale": sb("w_scale", [P, 2]),
            "b1_col": sb("b1_col", [P, ET]),
            "b2_row": sb("b2_row", [P, D]),
            "half4": sb("half4", [P, 4]),
        }
        keep["half"] = keep["half4"][:, 0:2]
        with ExitStack() as inner:
            def weight(name, shape, dt=F32):
                keep[name] = inner.enter_context(nc.sbuf_tensor(name, shape, dt))

            weight("causal", [P, P])
            weight("bo_row", [P, D])
            weight("g_bias", [P, DT])
            weight("qk_bias", [P, 1])
            weight("third", [P, 2, 3])
            weight("negs", [P, 2, 3])
            weight("fold_qk", [P, 2, DT, D], F32R)
            weight("fold_vo", [P, 2, DT, FW], F32R)
            for n in ("Wq", "Wk", "Wv"):
                weight("cross_" + n, [P, 2, DT, INNER], F32R)
            weight("cross_Wo", [P, 2, ET, D], F32R)
            prepare_weights(nc, dram, keep, psum)
            attentions(nc, dram, keep, psum, x2_dram)
        feed_forward(nc, keep, psum, x2_dram, out_dram)


NAMES = {"x": "x", "ctx_1024": "ctx", "fside_Bx1xSxS2_0": "mask"}
INS = ["x", "ctx_1024", "fside_Bx1xSxS2_0", "L0_attn_Wq", "L0_attn_bq", "L0_attn_Wk", "L0_attn_bk", "L0_attn_Wv",
       "L0_attn_bv", "L0_attn_Wo", "L0_attn_bo", "L0_xattn_Wq", "L0_xattn_Wk", "L0_xattn_Wv", "L0_xattn_Wo",
       "L0_ffn_w1", "L0_ffn_b1", "L0_ffn_w2", "L0_ffn_b2"]


def kernel(**inputs):
    import numpy as np
    import concourse.bacc as bacc
    from concourse.bass_utils import run_bass_kernel_spmd

    nc = bacc.Bacc("TRN2", target_bir_lowering=False, num_devices=1)
    arrays, dram = {}, {}
    for name in INS:
        a = np.ascontiguousarray(inputs[name])
        arrays[f"in_{name}_dram"] = a
        short = NAMES.get(name, name.removeprefix("L0_"))
        dram[short] = nc.dram_tensor(f"in_{name}_dram", a.shape, mybir.dt.from_np(a.dtype), kind="ExternalInput").ap()
    out = nc.dram_tensor("out_0_dram", (NB, P, D), F32, kind="ExternalOutput").ap()
    decoder_layer(nc, dram, out)
    r = run_bass_kernel_spmd(nc, [arrays], core_ids=[0])
    return r.results[0]["out_0_dram"]
```
